# Optimizing a Trainium2 kernel written in Bass

```python
import numpy as np
import jax
import jax.numpy as jnp

def _softmax(x, axis=-1):
    return jax.nn.softmax(x, axis=axis)

def _gelu(x):
    return jax.nn.gelu(x, approximate=True)

def _silu(x):
    return jax.nn.silu(x)

def _sigmoid(x):
    return jax.nn.sigmoid(x)

def _layernorm(x, axis=-1, eps=1e-05):
    m = jnp.mean(x, axis=axis, keepdims=True)
    v = jnp.var(x, axis=axis, keepdims=True)
    return (x - m) / jnp.sqrt(v + eps)

def _scatter_add(tgt, idx, src, axis=0):
    return tgt.at[idx].add(src)

def _segment_sum(src, seg, n):
    return jax.ops.segment_sum(src, seg, n)
kernel_name = 'mk_flamingo_gated_d2_seqx_r4_8d3de0'

def setup_inputs(seed: int=0):
    np.random.seed(seed)
    _w = jnp.asarray

    def _rec_inputs():
        import jax
        import jax.numpy as jnp
        _rk = jax.random.key(seed)
        x = 7.22e-05 + 1 * jax.random.normal(jax.random.fold_in(_rk, 1), (16, 256, 256), jnp.float32)
        _lenS = 256 - jax.random.randint(jax.random.fold_in(_rk, 7), (16,), 0, max(1, 256 // 4) + 1, jnp.int32)
        _lenS2 = 256 - jax.random.randint(jax.random.fold_in(_rk, 8), (16,), 0, max(1, 256 // 4) + 1, jnp.int32)
        _ctx_1024P = jax.random.normal(jax.random.fold_in(_rk, 11), (16, 16, 256), jnp.float32)
        _ctx_1024c = jax.random.dirichlet(jax.random.fold_in(_rk, 511), 0.3 * jnp.ones((16,), jnp.float32), (16, 256))
        _ctx_1024t = jnp.einsum('bsk,bkd->bsd', _ctx_1024c, _ctx_1024P)
        _ctx_1024t = _ctx_1024t * jax.lax.rsqrt(jnp.mean(jnp.square(_ctx_1024t)) + 1e-12) * 0.953939
        ctx_1024 = 4.13588e-05 + 0.999923 * (_ctx_1024t + 0.3 * jax.random.normal(jax.random.fold_in(_rk, 611), (16, 256, 256), jnp.float32))
        _g = jax.random.normal(jax.random.fold_in(_rk, 9001), (2, 2), jnp.float32)
        _g = jnp.sign(_g) * jnp.maximum(jnp.abs(_g), 1.0) + (_g == 0) * 1.0
        g_xattn = _g[0]
        g_ffn = _g[1]
        return (x, ctx_1024, g_xattn, g_ffn)
    x, ctx_1024, g_xattn, g_ffn = _rec_inputs()

    def _L0_xattn_setup():
        import jax, jax.numpy as jnp
        import numpy as np
        EMBED_DIM = 256
        HEAD_DIM = 256
        GAMMA = 0.96875
        THETA = 10000.0
        SCALE_BASE = 512.0

        def _dup_interleave(x):
            return jnp.repeat(x, 2, axis=-1)

        def _rotate_half(x):
            x_even = x[..., ::2]
            x_odd = x[..., 1::2]
            return jnp.stack((-x_odd, x_even), axis=-1).reshape(x.shape)

        def _xpos(x, offset=0, inverse_scale=False):
            l = x.shape[-2]
            half = HEAD_DIM // 2
            scale_vec = (jnp.arange(0, HEAD_DIM, 2, dtype=jnp.float32) + 0.4 * HEAD_DIM) / (1.4 * HEAD_DIM)
            pos = jnp.arange(offset, offset + l, dtype=jnp.float32)
            scale = scale_vec[None, :] ** (pos / SCALE_BASE)[:, None]
            freqs = 1.0 / THETA ** (jnp.arange(half, dtype=jnp.float32) / half)
            sin_in = pos[:, None] * freqs[None, :]
            sin, cos = (jnp.sin(sin_in), jnp.cos(sin_in))
            if inverse_scale:
                scale = 1.0 / scale
            return x * _dup_interleave(cos * scale) + _rotate_half(x) * _dup_interleave(sin * scale)

        def _decay_mask(l, gamma):
            idx = jnp.arange(l, dtype=jnp.float32)
            diff = idx[:, None] - idx[None, :]
            return jnp.where(diff >= 0, gamma ** diff, 0.0)
        key = jax.random.key(seed)
        k1, k2, k3, k4, k5, k6 = jax.random.split(key, 6)
        B, L = (4, 512)
        s = 1.0 / np.sqrt(EMBED_DIM)
        return {'q': jax.random.normal(k1, (B, L, EMBED_DIM), dtype=jnp.float32), 'k': jax.random.normal(k2, (B, L, EMBED_DIM), dtype=jnp.float32), 'v': jax.random.normal(k3, (B, L, EMBED_DIM), dtype=jnp.float32), 'Wq': jax.random.normal(k4, (EMBED_DIM, HEAD_DIM), dtype=jnp.float32) * s, 'Wk': jax.random.normal(k5, (EMBED_DIM, HEAD_DIM), dtype=jnp.float32) * s, 'Wv': jax.random.normal(k6, (EMBED_DIM, HEAD_DIM), dtype=jnp.float32) * s}
    _L0_xattn_all = _L0_xattn_setup()
    _L0_xattn_in = {k: v for k, v in _L0_xattn_all.items() if k in ('Wq', 'Wk', 'Wv')}
    del _L0_xattn_all

    def _L0_ffn_setup():
        import jax, jax.numpy as jnp
        import numpy as np
        HIDDEN = 256
        MOE_INTER = 128
        SHARED_INTER = 512
        N_EXPERTS = 32
        TOP_K = 6
        N_GROUP = 8
        TOPK_GROUP = 4
        ROUTED_SCALE = 2.5

        def _relu2(x):
            return jnp.square(jax.nn.relu(x))

        def _router(x, gate_w, e_bias):
            T = x.shape[0]
            logits = x.astype(jnp.float32) @ gate_w.astype(jnp.float32).T
            scores = jax.nn.sigmoid(logits)
            sc = scores + e_bias[None, :]
            g = sc.reshape(T, N_GROUP, N_EXPERTS // N_GROUP)
            group_scores = jax.lax.top_k(g, 2)[0].sum(-1)
            group_idx = jax.lax.top_k(group_scores, TOPK_GROUP)[1]
            group_mask = jnp.zeros_like(group_scores).at[jnp.arange(T)[:, None], group_idx].set(1.0)
            score_mask = jnp.repeat(group_mask, N_EXPERTS // N_GROUP, axis=1)
            masked = jnp.where(score_mask > 0, sc, 0.0)
            topk_idx = jax.lax.stop_gradient(jax.lax.top_k(masked, TOP_K)[1])
            topk_w = jnp.take_along_axis(scores, topk_idx, axis=1)
            topk_w = topk_w / (topk_w.sum(-1, keepdims=True) + 1e-20)
            topk_w = topk_w * ROUTED_SCALE
            return (topk_idx, topk_w)
        if __name__ == '__main__':
            out = reference(**setup_inputs())
            print(out.shape, out.dtype)
        key = jax.random.key(seed)
        ks = jax.random.split(key, 6)
        s = 0.02
        return {'hidden_states': jax.random.normal(ks[0], (2, 256, HIDDEN), jnp.float32), 'gate_w': jax.random.normal(ks[1], (N_EXPERTS, HIDDEN), jnp.float32) * s, 'e_bias': jnp.zeros((N_EXPERTS,), jnp.float32), 'up_w': jax.random.normal(ks[2], (N_EXPERTS, MOE_INTER, HIDDEN), jnp.float32) * s, 'down_w': jax.random.normal(ks[3], (N_EXPERTS, HIDDEN, MOE_INTER), jnp.float32) * s, 'shared_up_w': jax.random.normal(ks[4], (SHARED_INTER, HIDDEN), jnp.float32) * s, 'shared_down_w': jax.random.normal(ks[5], (HIDDEN, SHARED_INTER), jnp.float32) * s}
    _L0_ffn_all = _L0_ffn_setup()
    _L0_ffn_in = {k: v for k, v in _L0_ffn_all.items() if k in ('gate_w', 'e_bias', 'up_w', 'down_w', 'shared_up_w', 'shared_down_w')}
    del _L0_ffn_all

    def _L1_xattn_setup():
        import jax, jax.numpy as jnp
        import numpy as np
        D_MODEL = 256
        NUM_HEADS = 16
        HEAD_DIM = D_MODEL // NUM_HEADS

        def _split_heads(x, B):
            return x.reshape(B, -1, NUM_HEADS, HEAD_DIM).transpose(0, 2, 1, 3)
        key = jax.random.key(seed)
        ks = jax.random.split(key, 11)
        B, S = (2, 512)
        s = 1.0 / np.sqrt(D_MODEL)
        inp = {'q': jax.random.normal(ks[0], (B, S, D_MODEL), jnp.float32), 'k': jax.random.normal(ks[1], (B, S, D_MODEL), jnp.float32), 'v': jax.random.normal(ks[2], (B, S, D_MODEL), jnp.float32), 'wq': jax.random.normal(ks[3], (D_MODEL, D_MODEL), jnp.float32) * s, 'bq': jnp.zeros((D_MODEL,), jnp.float32), 'wk': jax.random.normal(ks[4], (D_MODEL, D_MODEL), jnp.float32) * s, 'bk': jnp.zeros((D_MODEL,), jnp.float32), 'wv': jax.random.normal(ks[5], (D_MODEL, D_MODEL), jnp.float32) * s, 'bv': jnp.zeros((D_MODEL,), jnp.float32), 'wo': jax.random.normal(ks[6], (D_MODEL, D_MODEL), jnp.float32) * s, 'bo': jnp.zeros((D_MODEL,), jnp.float32)}
        return inp
    _L1_xattn_all = _L1_xattn_setup()
    _L1_xattn_in = {k: v for k, v in _L1_xattn_all.items() if k in ('wq', 'bq', 'wk', 'bk', 'wv', 'bv', 'wo', 'bo')}
    del _L1_xattn_all

    def _L1_ffn_setup():
        import jax, jax.numpy as jnp
        import numpy as np
        import math
        BETA = 0.9
        THRESHOLD = 1.0
        NUM_STEPS = 5
        ALPHA = 2.0

        @jax.custom_vjp
        def spike_fn(u):
            return (u > 0).astype(u.dtype)

        def _spike_fwd(u):
            return (spike_fn(u), u)

        def _spike_bwd(u, g):
            s = jnp.pi / 2.0 * ALPHA * u
            return (g * (ALPHA / 2.0) / (1.0 + s * s),)
        spike_fn.defvjp(_spike_fwd, _spike_bwd)
        key = jax.random.key(seed)
        k1, k2, k3 = jax.random.split(key, 3)
        n_embd = 256
        x = jax.random.normal(k1, (4, 512, n_embd), dtype=jnp.float32)
        W_fc = jax.random.normal(k2, (4 * n_embd, n_embd), dtype=jnp.float32) / math.sqrt(n_embd)
        W_proj = jax.random.normal(k3, (n_embd, 4 * n_embd), dtype=jnp.float32) / math.sqrt(4 * n_embd)
        return {'x': x, 'W_fc': W_fc, 'W_proj': W_proj}
    _L1_ffn_all = _L1_ffn_setup()
    _L1_ffn_in = {k: v for k, v in _L1_ffn_all.items() if k in ('W_fc', 'W_proj')}
    del _L1_ffn_all
    return {'x': x, 'ctx_1024': ctx_1024, 'g_xattn': g_xattn, 'g_ffn': g_ffn, 'L0_xattn_Wq': _L0_xattn_in['Wq'], 'L0_xattn_Wk': _L0_xattn_in['Wk'], 'L0_xattn_Wv': _L0_xattn_in['Wv'], 'L0_ffn_gate_w': _L0_ffn_in['gate_w'], 'L0_ffn_e_bias': _L0_ffn_in['e_bias'], 'L0_ffn_up_w': _L0_ffn_in['up_w'], 'L0_ffn_down_w': _L0_ffn_in['down_w'], 'L0_ffn_shared_up_w': _L0_ffn_in['shared_up_w'], 'L0_ffn_shared_down_w': _L0_ffn_in['shared_down_w'], 'L1_xattn_wq': _L1_xattn_in['wq'], 'L1_xattn_bq': _L1_xattn_in['bq'], 'L1_xattn_wk': _L1_xattn_in['wk'], 'L1_xattn_bk': _L1_xattn_in['bk'], 'L1_xattn_wv': _L1_xattn_in['wv'], 'L1_xattn_bv': _L1_xattn_in['bv'], 'L1_xattn_wo': _L1_xattn_in['wo'], 'L1_xattn_bo': _L1_xattn_in['bo'], 'L1_ffn_W_fc': _L1_ffn_in['W_fc'], 'L1_ffn_W_proj': _L1_ffn_in['W_proj']}

def reference(x, ctx_1024, g_xattn, g_ffn, L0_xattn_Wq, L0_xattn_Wk, L0_xattn_Wv, L0_ffn_gate_w, L0_ffn_e_bias, L0_ffn_up_w, L0_ffn_down_w, L0_ffn_shared_up_w, L0_ffn_shared_down_w, L1_xattn_wq, L1_xattn_bq, L1_xattn_wk, L1_xattn_bk, L1_xattn_wv, L1_xattn_bv, L1_xattn_wo, L1_xattn_bo, L1_ffn_W_fc, L1_ffn_W_proj):
    import jax
    import jax.numpy as jnp

    def _L0_xattn_ref(q, k, v, Wq, Wk, Wv):
        import jax, jax.numpy as jnp
        import numpy as np
        EMBED_DIM = 256
        HEAD_DIM = 256
        GAMMA = 0.96875
        THETA = 10000.0
        SCALE_BASE = 512.0

        def _dup_interleave(x):
            return jnp.repeat(x, 2, axis=-1)

        def _rotate_half(x):
            x_even = x[..., ::2]
            x_odd = x[..., 1::2]
            return jnp.stack((-x_odd, x_even), axis=-1).reshape(x.shape)

        def _xpos(x, offset=0, inverse_scale=False):
            l = x.shape[-2]
            half = HEAD_DIM // 2
            scale_vec = (jnp.arange(0, HEAD_DIM, 2, dtype=jnp.float32) + 0.4 * HEAD_DIM) / (1.4 * HEAD_DIM)
            pos = jnp.arange(offset, offset + l, dtype=jnp.float32)
            scale = scale_vec[None, :] ** (pos / SCALE_BASE)[:, None]
            freqs = 1.0 / THETA ** (jnp.arange(half, dtype=jnp.float32) / half)
            sin_in = pos[:, None] * freqs[None, :]
            sin, cos = (jnp.sin(sin_in), jnp.cos(sin_in))
            if inverse_scale:
                scale = 1.0 / scale
            return x * _dup_interleave(cos * scale) + _rotate_half(x) * _dup_interleave(sin * scale)

        def _decay_mask(l, gamma):
            idx = jnp.arange(l, dtype=jnp.float32)
            diff = idx[:, None] - idx[None, :]
            return jnp.where(diff >= 0, gamma ** diff, 0.0)
        qh = _xpos(q @ Wq, offset=0, inverse_scale=False)
        kh = _xpos(k @ Wk, offset=0, inverse_scale=True)
        vh = v @ Wv
        L = qh.shape[-2]
        mask = _decay_mask(L, GAMMA)
        scores = jnp.einsum('bld,bmd->blm', qh, kh) * mask[None, :, :]
        return scores @ vh

    def _L0_ffn_ref(hidden_states, gate_w, e_bias, up_w, down_w, shared_up_w, shared_down_w):
        import jax, jax.numpy as jnp
        import numpy as np
        HIDDEN = 256
        MOE_INTER = 128
        SHARED_INTER = 512
        N_EXPERTS = 32
        TOP_K = 6
        N_GROUP = 8
        TOPK_GROUP = 4
        ROUTED_SCALE = 2.5

        def _relu2(x):
            return jnp.square(jax.nn.relu(x))

        def _router(x, gate_w, e_bias):
            T = x.shape[0]
            logits = x.astype(jnp.float32) @ gate_w.astype(jnp.float32).T
            scores = jax.nn.sigmoid(logits)
            sc = scores + e_bias[None, :]
            g = sc.reshape(T, N_GROUP, N_EXPERTS // N_GROUP)
            group_scores = jax.lax.top_k(g, 2)[0].sum(-1)
            group_idx = jax.lax.top_k(group_scores, TOPK_GROUP)[1]
            group_mask = jnp.zeros_like(group_scores).at[jnp.arange(T)[:, None], group_idx].set(1.0)
            score_mask = jnp.repeat(group_mask, N_EXPERTS // N_GROUP, axis=1)
            masked = jnp.where(score_mask > 0, sc, 0.0)
            topk_idx = jax.lax.stop_gradient(jax.lax.top_k(masked, TOP_K)[1])
            topk_w = jnp.take_along_axis(scores, topk_idx, axis=1)
            topk_w = topk_w / (topk_w.sum(-1, keepdims=True) + 1e-20)
            topk_w = topk_w * ROUTED_SCALE
            return (topk_idx, topk_w)
        if __name__ == '__main__':
            out = reference(**setup_inputs())
            print(out.shape, out.dtype)
        B, S, H = hidden_states.shape
        x = hidden_states.reshape(-1, H)
        T = x.shape[0]
        topk_idx, topk_w = _router(x, gate_w, e_bias)
        combine = jnp.zeros((T, N_EXPERTS), topk_w.dtype).at[jnp.arange(T)[:, None], topk_idx].add(topk_w)
        h = _relu2(jnp.einsum('th,eih->tei', x, up_w))
        h = h * combine[:, :, None]
        moe_out = jnp.einsum('tei,ehi->th', h, down_w)
        shared = _relu2(x @ shared_up_w.T) @ shared_down_w.T
        return (moe_out + shared).reshape(B, S, H)

    def _L1_xattn_ref(q, k, v, wq, bq, wk, bk, wv, bv, wo, bo):
        import jax, jax.numpy as jnp
        import numpy as np
        D_MODEL = 256
        NUM_HEADS = 16
        HEAD_DIM = D_MODEL // NUM_HEADS

        def _split_heads(x, B):
            return x.reshape(B, -1, NUM_HEADS, HEAD_DIM).transpose(0, 2, 1, 3)
        B = q.shape[0]
        qh = _split_heads(q @ wq + bq, B)
        kh = _split_heads(k @ wk + bk, B)
        vh = _split_heads(v @ wv + bv, B)
        scale = 1.0 / np.sqrt(HEAD_DIM).astype(np.float32)
        scores = jnp.einsum('bhqd,bhkd->bhqk', qh, kh) * scale
        probs = jax.nn.softmax(scores, axis=-1)
        out = jnp.einsum('bhqk,bhkd->bhqd', probs, vh)
        out = out.transpose(0, 2, 1, 3).reshape(B, -1, D_MODEL)
        return out @ wo + bo

    def _L1_ffn_ref(x, W_fc, W_proj):
        import jax, jax.numpy as jnp
        import numpy as np
        import math
        BETA = 0.9
        THRESHOLD = 1.0
        NUM_STEPS = 5
        ALPHA = 2.0

        @jax.custom_vjp
        def spike_fn(u):
            return (u > 0).astype(u.dtype)

        def _spike_fwd(u):
            return (spike_fn(u), u)

        def _spike_bwd(u, g):
            s = jnp.pi / 2.0 * ALPHA * u
            return (g * (ALPHA / 2.0) / (1.0 + s * s),)
        spike_fn.defvjp(_spike_fwd, _spike_bwd)
        h = jnp.square(jax.nn.relu(jnp.einsum('bsd,fd->bsf', x, W_fc)))
        y = jnp.einsum('bsf,df->bsd', h, W_proj)

        def step(mem, _):
            reset = jax.lax.stop_gradient(spike_fn(mem - THRESHOLD))
            mem_new = BETA * mem + y - reset * THRESHOLD
            spk = spike_fn(mem_new - THRESHOLD)
            return (mem_new, spk)
        mem0 = jnp.zeros_like(y)
        _, spks = jax.lax.scan(step, mem0, None, length=NUM_STEPS)
        return jnp.sum(spks, axis=0) / NUM_STEPS
    x = x + jnp.tanh(g_xattn[0]) * _L0_xattn_ref(_layernorm(x, axis=-1), ctx_1024, ctx_1024, L0_xattn_Wq, L0_xattn_Wk, L0_xattn_Wv)
    x = x + jnp.tanh(g_ffn[0]) * _L0_ffn_ref(_layernorm(x, axis=-1), L0_ffn_gate_w, L0_ffn_e_bias, L0_ffn_up_w, L0_ffn_down_w, L0_ffn_shared_up_w, L0_ffn_shared_down_w)
    x = x + jnp.tanh(g_xattn[1]) * _L1_xattn_ref(_layernorm(x, axis=-1), ctx_1024, ctx_1024, L1_xattn_wq, L1_xattn_bq, L1_xattn_wk, L1_xattn_bk, L1_xattn_wv, L1_xattn_bv, L1_xattn_wo, L1_xattn_bo)
    x = x + jnp.tanh(g_ffn[1]) * _L1_ffn_ref(_layernorm(x, axis=-1), L1_ffn_W_fc, L1_ffn_W_proj)
    return x

_drawn_inputs = setup_inputs


def setup_inputs(seed=0):
    import zlib

    import numpy as np

    out = dict(_drawn_inputs(seed))
    spreads = {'g_ffn': (-1.0, 0.6),
     'L0_ffn_e_bias': (0.0, 0.8),
     'L1_xattn_bq': (0.0, 0.8),
     'L1_xattn_bk': (0.0, 0.8),
     'L1_xattn_bv': (0.0, 0.8),
     'L1_xattn_bo': (0.0, 0.8)}
    factors = {'L0_ffn_gate_w': 8.0,
     'L0_ffn_up_w': 8.0,
     'L0_ffn_down_w': 8.0,
     'L0_ffn_shared_up_w': 8.0,
     'L0_ffn_shared_down_w': 8.0,
     'L1_xattn_wq': 8.0,
     'L1_xattn_wk': 8.0,
     'L1_xattn_wv': 8.0,
     'L1_xattn_wo': 8.0,
     'L1_ffn_W_fc': 8.0,
     'L1_ffn_W_proj': 8.0}
    for name, (base, spread) in spreads.items():
        noise = np.random.default_rng([zlib.crc32(name.encode()), seed]).standard_normal(out[name].shape)
        drawn = base * np.exp(spread * noise) if base else spread * noise
        out[name] = jnp.asarray(drawn.astype(out[name].dtype))
    for name, factor in factors.items():
        out[name] = (out[name] * factor).astype(out[name].dtype)
    return out
```

```python
from contextlib import ExitStack

import numpy as np

import concourse.bass as bass
from concourse import mybir

F32 = mybir.dt.float32
F16 = mybir.dt.float16
ALU = mybir.AluOpType
ACT = mybir.ActivationFunctionType
AX_X = mybir.AxisListType.X

P = 128
NB, SEQ, D = 16, 256, 256
DT = D // P
PAIR = 2
T = PAIR * SEQ
TT = T // P
GROUPS = NB // PAIR
EXPERTS, SHARED = 32, 4
CHUNKS = EXPERTS + SHARED
FC = 8
TOP_GROUPS, TOP_K = 4, 6
EXPERT_GROUPS = 8
ROUTED_SCALE = 2.5
HEADS, HD = 16, 16
STEPS, BETA, THRESHOLD = 5, 0.9, 1.0
EPS = 1e-5

SX = 16.0
SW = 256.0
SR = 8.0
SV = 16.0
SM = 16.0
SF = 1.0 / 16.0
BIG = 1.0e30

WEIGHTS = {}
WCOLS = 0
for _name, _n in (("wq0", DT * D), ("wk0", DT * D), ("wv0", DT * D), ("gate", DT * EXPERTS),
                  ("up", CHUNKS * DT * P), ("down", CHUNKS * D),
                  ("wq1", DT * D), ("wk1", DT * D), ("wv1", DT * D), ("wo", 4 * D),
                  ("fc", FC * DT * P), ("proj", FC * D)):
    WEIGHTS[_name] = (WCOLS, _n)
    WCOLS += _n
STAGE = 992
STAGES = 3
PIECES = -(-WCOLS // STAGE)
PIECES += -PIECES % STAGES
WCOLS = PIECES * STAGE

CONSTS = {}
CCOLS = 0
for _name, _n in (("ident", P), ("cq", SEQ), ("sq", SEQ), ("ck", SEQ), ("sk", SEQ),
                  ("decay", 2 * SEQ), ("den", P), ("pick", EXPERTS)):
    CONSTS[_name] = (CCOLS, _n)
    CCOLS += _n


HEAD = 4


class Signal:

    def __init__(self, sem, events):
        self.sem = sem
        self.events = list(events)

    def at(self, g, event):
        return HEAD + g * len(self.events) + self.events.index(event) + 1


def wait(eng, sem, value):
    if not isinstance(value, int) or value > 0:
        eng.wait_ge(sem, value)


class Banks:

    def __init__(self, banks, full, read, steps):
        self.banks, self.full, self.read, self.steps = banks, full, read, list(steps)

    def bank(self, step):
        return self.banks[self.steps.index(step) % len(self.banks)]

    def reader(self, step):
        return self.read[self.steps.index(step) % len(self.banks)]

    def full_at(self, g, step):
        return g * len(self.steps) + self.steps.index(step) + 1

    def read_at(self, g, step, done=1):
        k, n = self.steps.index(step), len(self.banks)
        return HEAD + g * len(range(k % n, len(self.steps), n)) + k // n + done

    def wait_free(self, eng, g, step):
        wait(eng, self.reader(step), self.read_at(g, step, 0))

    def wait_full(self, eng, g, step):
        eng.wait_ge(self.full, self.full_at(g, step))

    def wait_read(self, eng, g, step):
        eng.wait_ge(self.reader(step), self.read_at(g, step))


def constants():
    c = np.zeros((P, CCOLS), np.float32)

    def put(name, a):
        o, n = CONSTS[name]
        c[:a.shape[0], o:o + n] = a.reshape(a.shape[0], n)

    half = D // 2
    scale_vec = (np.arange(0, D, 2, dtype=np.float32) + np.float32(0.4 * D)) / np.float32(1.4 * D)
    pos = np.arange(SEQ, dtype=np.float32)
    scale = scale_vec[None, :] ** (pos / np.float32(512.0))[:, None]
    freqs = np.float32(1.0) / np.float32(10000.0) ** (np.arange(half, dtype=np.float32) / np.float32(half))
    angle = pos[:, None] * freqs[None, :]
    undo = np.float32(SR / (SX * SW))
    put("cq", (np.cos(angle) * scale * undo).T)
    put("sq", (np.sin(angle) * scale * undo).T)
    put("ck", (np.cos(angle) * (1.0 / scale) * undo).T)
    put("sk", (np.sin(angle) * (1.0 / scale) * undo).T)
    key = np.arange(P)[:, None, None] + P * np.arange(2)[None, :, None]
    gap = np.arange(SEQ)[None, None, :] - key
    put("decay", np.where(gap >= 0, np.float32(0.96875) ** gap.astype(np.float32), 0) / (SR * SR))
    put("ident", np.eye(P))
    den = np.zeros((P, P))
    den[32 * (np.arange(P) // 32) + HD, np.arange(P)] = 1
    put("den", den)
    pick = np.zeros((P, EXPERTS))
    pick[np.arange(64), np.arange(64) % 32] = 1
    put("pick", pick)
    return c


def build(nc, x, ctx, gates, weights, consts, ebias, bqk, bv, bo, x_mid, out):
    with ExitStack() as whole:
        sem = lambda name: whole.enter_context(nc.semaphore(name))
        psum = [whole.enter_context(nc.psum_tensor(f"bank{b}", [P, 512], F32)) for b in range(8)]

        def sb(name, shape, dt=F32, to=whole):
            return to.enter_context(nc.sbuf_tensor(name, shape, dt))

        w_hi = sb("w_hi", [P, WCOLS], F16)
        w_lo = sb("w_lo", [P, WCOLS], F16)
        table = sb("table", [P, CCOLS])
        pick16 = sb("pick16", [P, EXPERTS], F16)
        minus_half = sb("minus_half", [P, TT])
        gate_in = sb("gate_in", [P, 4])
        tanh_g = sb("tanh_g", [P, 4])
        step_of = sb("step_of", [P, 4])
        bias_e = sb("bias_e", [P, EXPERTS])
        bias_qk = sb("bias_qk", [P, 4])
        bias_v = sb("bias_v", [P, D])
        bias_o = sb("bias_o", [P, D])

        def const(name):
            o, n = CONSTS[name]
            return table[:, o:o + n]

        def weight(part, name, start, n):
            o = WEIGHTS[name][0] + start
            return part[:, o:o + n]

        ident = const("ident")

        loaded = [sem(f"weights_loaded{i}") for i in range(STAGES)]
        consts_in = sem("consts_in")
        tanh_done = sem("tanh_done")
        setup_done = sem("setup_done")
        rounded = sem("weights_rounded")
        split = sem("weights_split")

        with ExitStack() as first:
            stage = sb("stage", [P, STAGES, STAGE], to=first)
            block = first.enter_context(nc.Block())

            @block.sync
            def _(sp):
                for t, src in ((table[:, :], consts), (bias_qk[:, :], bqk),
                               (bias_e[:, :], ebias.partition_broadcast(P)),
                               (bias_v[:, :], bv.partition_broadcast(P)),
                               (bias_o[:, :], bo.partition_broadcast(P)),
                               (gate_in[:, :], gates.partition_broadcast(P))):
                    sp.dma_start(t, src).then_inc(consts_in, 16)
                for s in range(STAGES):
                    sp.dma_start(stage[:, s, :], weights[:, s * STAGE:(s + 1) * STAGE]).then_inc(loaded[s], 16)
                with sp.Fori(1, PIECES // STAGES) as i:
                    for s in range(STAGES):
                        sp.wait_ge(split, i * STAGES + s - STAGES + 1)
                        sp.dma_start(stage[:, s, :], weights[:, bass.ds(i * (STAGES * STAGE) + s * STAGE, STAGE)]) \
                          .then_inc(loaded[s], 16)

            @block.scalar
            def _(act):
                act.wait_ge(consts_in, 6 * 16)
                nc.scalar.activation(tanh_g[:, :], gate_in[:, :], ACT.Tanh).then_inc(tanh_done, 1)
                with act.Fori(0, PIECES // STAGES) as i:
                    for s in range(STAGES):
                        act.wait_ge(loaded[s], i * 16 + 16)
                        nc.scalar.activation(w_hi[:, bass.ds(i * (STAGES * STAGE) + s * STAGE, STAGE)], stage[:, s, :],
                                             ACT.Copy, scale=SW).then_inc(rounded, 1)

            @block.vector
            def _(dve):
                nc.vector.memset(minus_half[:, :], -0.5).then_inc(setup_done, 1)
                dve.wait_ge(consts_in, 6 * 16)
                nc.vector.tensor_copy(pick16[:, :], const("pick")).then_inc(setup_done, 1)
                dve.wait_ge(tanh_done, 1)
                for k, undo in enumerate((1 / SV, 1 / SW, 1.0, 1 / STEPS)):
                    nc.vector.tensor_scalar(step_of[:, k:k + 1], tanh_g[:, k:k + 1], undo, None, ALU.mult) \
                      .then_inc(setup_done, 1)
                with dve.Fori(0, PIECES // STAGES) as i:
                    for s in range(STAGES):
                        dve.wait_ge(rounded, i * STAGES + s + 1)
                        nc.vector.scalar_tensor_tensor(
                            out=w_lo[:, bass.ds(i * (STAGES * STAGE) + s * STAGE, STAGE)], in0=stage[:, s, :], scalar=SW,
                            in1=w_hi[:, bass.ds(i * (STAGES * STAGE) + s * STAGE, STAGE)],
                            op0=ALU.mult, op1=ALU.subtract).then_inc(split, 1)

        def parts3(a_hi, a_lo, b_hi, b_lo):
            return ((a_hi, b_hi), (a_hi, b_lo), (a_lo, b_hi))

        def product(pe, dst, pairs):
            todo = [ab for a_hi, a_lo, b_hi, b_lo in pairs for ab in parts3(a_hi, a_lo, b_hi, b_lo)]
            for n, (a, b) in enumerate(todo):
                mm = pe.matmul(dst, a, b, start=n == 0, stop=n == len(todo) - 1)
            return mm

        def transposes(pe, bank, src, dt):
            for tt in range(TT):
                mm = pe.transpose(bank[:, tt * P:(tt + 1) * P], src[:, tt, dt * P:(dt + 1) * P], ident)
            return mm

        with ExitStack() as first:
            x_tok = [sb(f"x_tok{p}", [P, TT, D], to=first) for p in range(2)]
            ctx_tok = sb("ctx_tok", [P, TT, D], to=first)
            xn = sb("xn", [P, TT, D], to=first)
            stats = sb("stats", [P, TT, 6], to=first)
            moments = sb("moments", [P, TT, 2], to=first)
            var_eps = sb("var_eps", [P, TT], to=first)
            rstd = sb("rstd", [P, TT], to=first)
            xt_hi, xt_lo = (sb(f"xt_{n}", [P, DT, T], F16, first) for n in ("hi", "lo"))
            ct_hi, ct_lo = (sb(f"ct_{n}", [P, DT, T], F16, first) for n in ("hi", "lo"))
            rot = {s: sb(f"rot_{s}", [P, 4, T], to=first) for s in "qk"}
            rot_hi = {s: sb(f"rot_hi_{s}", [P, 2, T], F16, first) for s in "qk"}
            rot_lo = {s: sb(f"rot_lo_{s}", [P, 2, T], F16, first) for s in "qk"}
            v_hi, v_lo = (sb(f"v_{n}", [P, TT, D], F16, first) for n in ("hi", "lo"))
            sc_f = rot["q"][:, 2:4, :].rearrange("p b (k q) -> p b k q", k=2)
            sc_hi, sc_lo = (sb(f"sc_{n}", [P, PAIR, 2, SEQ], F16, first) for n in ("hi", "lo"))
            xf_hi, xf_lo = ([sb(f"xf_{n}{p}", [P, DT, T], F16, first) for p in range(2)] for n in ("hi", "lo"))
            logit_t = sb("logit_t", [EXPERTS, T], to=first)
            expo = sb("expo", [P, TT, EXPERTS], to=first)
            score = sb("score", [P, TT, EXPERTS], to=first)
            biased = sb("biased", [P, TT, EXPERTS], to=first)
            pair_hi = sb("pair_hi", [P, TT * EXPERT_GROUPS, 2], to=first)
            pair_lo = sb("pair_lo", [P, TT * EXPERT_GROUPS, 2], to=first)
            best = sb("best", [P, 3, TT * EXPERT_GROUPS], to=first)
            g_pad = sb("g_pad", [P, TT, 12], to=first)
            g_out = sb("g_out", [P, TT, 12], to=first)
            top8 = sb("top8", [P, TT, 8], to=first)
            g_mask = sb("g_mask", [P, TT, EXPERT_GROUPS], to=first)
            e_pad = sb("e_pad", [P, TT, EXPERTS + 2], to=first)
            e_out = sb("e_out", [P, TT, EXPERTS + 2], to=first)
            chosen = sb("chosen", [P, TT, EXPERTS], to=first)
            total = sb("total", [P, TT], to=first)
            combine = sb("combine", [P, TT, EXPERTS], to=first)
            comb_t = [sb(f"comb_t{p}", [96, T], F16, first) for p in range(2)]
            relu = sb("relu", [P, 2, T], to=first)
            gated = sb("gated", [P, 2, T], to=first)
            hid = sb("hid", [P, 3, T], to=first)
            hid_hi, hid_lo = (sb(f"hid_{n}", [P, 3, T], F16, first) for n in ("hi", "lo"))

            acc, hbank, cbank = psum[0:2], psum[2:4], psum[4]
            STEP0 = ["ctx0", "ctx1", "k0", "k1", "v0", "v1", "x0", "x1", "q0", "q1", "s0", "s1", "o0", "o1",
                     "f0", "f1", "logits", "logits_t", "comb_t"]
            FILL = {"ctx0": 0, "ctx1": 0, "k0": 2, "k1": 3, "v0": 4, "v1": 5, "x0": 7, "x1": 7, "q0": 9, "q1": 10,
                    "s0": 14, "s1": 15, "o0": 18, "o1": 19, "f0": 23, "f1": 23, "logits": 25, "logits_t": 27,
                    "comb_t": 35}
            ring = Banks(psum[5:8], sem("a_bank_full"), [sem(f"a_bank_read{b}") for b in range(3)], STEP0)
            x_in = [sem(f"a_x_in{p}") for p in range(2)]
            x_out = [sem(f"a_x_out{p}") for p in range(2)]
            ctx_in = sem("a_ctx_in")
            norm = Signal(sem("a_norm"), [f"{n}{k}" for k in range(2) for n in ("var", "xn")])
            rsqrt = Signal(sem("a_rsqrt"), ["0", "1"])
            hi_done = Signal(sem("a_hi_done"), ["ctx0", "ctx1", "v0", "k", "v1", "x0", "x1", "q", "s0", "s1",
                                                "f0", "f1", "comb"])
            lo_done = Signal(sem("a_lo_done"), ["k", "q", "s0", "s1"])
            turned = Signal(sem("a_turned"), ["k", "q"])
            combined = Signal(sem("a_combined"), [0])
            preset = sem("a_preset")
            waited = sem("a_waited")
            up_done = Signal(sem("a_up_done"), range(CHUNKS))
            relu_done = Signal(sem("a_relu_done"), range(CHUNKS))
            cb_done = Signal(sem("a_cb_done"), range(EXPERTS))
            gated_done = Signal(sem("a_gated_done"), range(EXPERTS))
            hid_done = Signal(sem("a_hid_done"), range(CHUNKS))
            hid_hi_done = Signal(sem("a_hid_hi_done"), range(CHUNKS))
            hid_lo_done = Signal(sem("a_hid_lo_done"), range(CHUNKS))
            down_done = Signal(sem("a_down_done"), range(CHUNKS))
            x_done = Signal(sem("a_x_done"), [0, 1])

            def previous(sig, g, k):
                return HEAD + g * len(sig.events) + k + 1

            block = first.enter_context(nc.Block())

            def attend_sp(sp, i, j):
                p = j
                wait(sp, x_out[p], 16 * i)
                sp.dma_start(x_tok[p][:, :, :], x[2 * i + j]).then_inc(x_in[p], 16)
                g = 2 * i + j
                if not isinstance(g, int) or g > 0:
                    ring.wait_full(sp, g - 1, "ctx1")
                sp.dma_start(ctx_tok[:, :, :], ctx[2 * i + j]).then_inc(ctx_in, 16)

            def attend_pe(pe, i, j):
                p, g = j, 2 * i + j

                def fill(step):
                    ring.wait_free(pe, g, step)
                    return ring.bank(step)

                def project(s, a_hi, a_lo, src):
                    for m in range(2):
                        yield FILL[f"{s}{m}"]
                        b = fill(f"{s}{m}")
                        for dt in range(DT):
                            ring.wait_read(pe, g, f"{src}{dt}")
                        product(pe, b[:, :], [(weight(w_hi, f"w{s}0", dt * D + m * P, P),
                                               weight(w_lo, f"w{s}0", dt * D + m * P, P),
                                               a_hi[:, dt, :], a_lo[:, dt, :]) for dt in range(DT)]) \
                            .then_inc(ring.full, 1)

                yield FILL["ctx0"]
                pe.wait_ge(ctx_in, 16 * (g + 1))
                for dt in range(DT):
                    transposes(pe, fill(f"ctx{dt}"), ctx_tok, dt).then_inc(ring.full, 1)
                yield from project("k", ct_hi, ct_lo, "ctx")
                for n in range(2):
                    yield FILL[f"v{n}"]
                    b = fill(f"v{n}")
                    for half in range(2):
                        tt = 2 * n + half
                        mm = product(pe, b[:, half * D:(half + 1) * D],
                                     [(ct_hi[:, dt, tt * P:(tt + 1) * P], ct_lo[:, dt, tt * P:(tt + 1) * P],
                                       weight(w_hi, "wv0", dt * D, D), weight(w_lo, "wv0", dt * D, D))
                                      for dt in range(DT)])
                    mm.then_inc(ring.full, 1)
                yield FILL["x0"]
                pe.wait_ge(norm.sem, norm.at(g, "xn0"))
                for dt in range(DT):
                    transposes(pe, fill(f"x{dt}"), xn, dt).then_inc(ring.full, 1)
                yield from project("q", xt_hi, xt_lo, "x")
                for b in range(PAIR):
                    yield FILL[f"s{b}"]
                    bank = fill(f"s{b}")
                    pe.wait_ge(lo_done.sem, lo_done.at(g, "q"))
                    for kt in range(2):
                        k0 = b * SEQ + kt * P
                        mm = product(pe, bank[:, kt * SEQ:(kt + 1) * SEQ],
                                     [(rot_hi["k"][:, m, k0:k0 + P], rot_lo["k"][:, m, k0:k0 + P],
                                       rot_hi["q"][:, m, b * SEQ:(b + 1) * SEQ],
                                       rot_lo["q"][:, m, b * SEQ:(b + 1) * SEQ]) for m in range(2)])
                    mm.then_inc(ring.full, 1)
                for b in range(PAIR):
                    yield FILL[f"o{b}"]
                    bank = fill(f"o{b}")
                    ring.wait_read(pe, g, f"v{b}")
                    pe.wait_ge(lo_done.sem, lo_done.at(g, f"s{b}"))
                    for qt in range(2):
                        mm = product(pe, bank[:, qt * D:(qt + 1) * D],
                                     [(sc_hi[:, b, kt, qt * P:(qt + 1) * P], sc_lo[:, b, kt, qt * P:(qt + 1) * P],
                                       v_hi[:, 2 * b + kt, :], v_lo[:, 2 * b + kt, :]) for kt in range(qt + 1)])
                    mm.then_inc(ring.full, 1)
                yield FILL["f0"]
                pe.wait_ge(norm.sem, norm.at(g, "xn1"))
                for dt in range(DT):
                    transposes(pe, fill(f"f{dt}"), xn, dt).then_inc(ring.full, 1)
                yield FILL["logits"]
                bank = fill("logits")
                for dt in range(DT):
                    ring.wait_read(pe, g, f"f{dt}")
                product(pe, bank[0:EXPERTS, :], [(weight(w_hi, "gate", dt * EXPERTS, EXPERTS),
                                                  weight(w_lo, "gate", dt * EXPERTS, EXPERTS),
                                                  xf_hi[p][:, dt, :], xf_lo[p][:, dt, :]) for dt in range(DT)]) \
                    .then_inc(ring.full, 1)
                yield FILL["logits_t"]
                bank = fill("logits_t")
                ring.wait_read(pe, g, "logits")
                pe.sem_inc(waited, 1)
                for tt in range(TT):
                    mm = pe.transpose(bank[:, tt * EXPERTS:(tt + 1) * EXPERTS], logit_t[:, tt * P:(tt + 1) * P],
                                      ident[0:EXPERTS, 0:EXPERTS])
                mm.then_inc(ring.full, 1)
                yield FILL["comb_t"]
                bank = fill("comb_t")
                pe.wait_ge(combined.sem, combined.at(g, 0))
                for tt in range(TT):
                    mm = pe.transpose(bank[0:EXPERTS, tt * P:(tt + 1) * P], combine[:, tt, :], ident)
                mm.then_inc(ring.full, 1)

            def attend_act(act, i, j):
                p, g = j, 2 * i + j

                def high(step, hi, scale):
                    yield FILL[step]
                    ring.wait_full(act, g, step)
                    nc.scalar.activation(hi, ring.bank(step)[:, :], ACT.Copy, scale=scale).then_inc(hi_done.sem, 1)

                def high_turned(s):
                    act.wait_ge(turned.sem, turned.at(g, s))
                    nc.scalar.activation(rot_hi[s][:, :, :], rot[s][:, 0:2, :], ACT.Copy).then_inc(hi_done.sem, 1)

                for dt in range(DT):
                    yield from high(f"ctx{dt}", ct_hi[:, dt, :], SX)
                yield from high("v0", v_hi[:, 0:2, :], SV / (SX * SW))
                yield FILL["k1"] + 2
                high_turned("k")
                yield from high("v1", v_hi[:, 2:4, :], SV / (SX * SW))
                for dt in range(DT):
                    yield from high(f"x{dt}", xt_hi[:, dt, :], SX)
                yield FILL["q1"] + 2
                high_turned("q")
                for b in range(PAIR):
                    yield FILL[f"s{b}"] + 1
                    ring.wait_read(act, g, f"s{b}")
                    nc.scalar.activation(sc_hi[:, b, :, :], sc_f[:, b, :, :], ACT.Copy).then_inc(hi_done.sem, 1)
                for dt in range(DT):
                    yield from high(f"f{dt}", xf_hi[p][:, dt, :], SX)
                yield FILL["logits_t"]
                ring.wait_full(act, g, "logits_t")
                nc.scalar.activation(expo[:, :, :], ring.bank("logits_t")[:, 0:TT * EXPERTS], ACT.Exp) \
                  .then_inc(ring.reader("logits_t"), 1)
                yield FILL["comb_t"]
                ring.wait_full(act, g, "comb_t")
                nc.scalar.activation(comb_t[p][0:EXPERTS, :], ring.bank("comb_t")[0:EXPERTS, :], ACT.Copy) \
                  .then_inc(hi_done.sem, 1)

            def moments_of(dve, sig, src):
                for tt in range(TT):
                    nc.vector.bn_stats(stats[:, tt, :], src[:, tt, :])
                dve.drain()
                for tt in range(TT):
                    nc.vector.bn_aggr(moments[:, tt, :], stats[:, tt, :])
                dve.drain()
                nc.vector.tensor_scalar(var_eps[:, :], moments[:, :, 1], EPS, None, ALU.add).then_inc(sig.sem, 1)

            def normalise(dve, sig, k, rs, g, src):
                dve.wait_ge(rs.sem, rs.at(g, f"{k}"))
                for tt in range(TT):
                    ins = nc.vector.tensor_scalar(xn[:, tt, :], src[:, tt, :], moments[:, tt, 0:1], rstd[:, tt:tt + 1],
                                                  ALU.subtract, ALU.mult)
                ins.then_inc(sig.sem, 1)

            def low_of_bank(dve, rg, sig, g, step, key, hi, lo, scale, cols=slice(None), rows=slice(None)):
                dve.wait_ge(sig.sem, sig.at(g, key))
                nc.vector.scalar_tensor_tensor(out=lo, in0=rg.bank(step)[rows, cols], scalar=scale, in1=hi,
                                               op0=ALU.mult, op1=ALU.subtract).then_inc(rg.reader(step), 1)

            def attend_dve(dve, i, j):
                p, g = j, 2 * i + j

                def low(step, hi, lo, scale):
                    yield FILL[step]
                    low_of_bank(dve, ring, hi_done, g, step, step, hi, lo, scale)

                def turn(s):
                    cos = const(f"c{s}").unsqueeze(1).to_broadcast([P, PAIR, SEQ])
                    sin = const(f"s{s}").unsqueeze(1).to_broadcast([P, PAIR, SEQ])
                    for m, (fa, fb) in enumerate(((cos, sin), (sin, cos))):
                        yield FILL[f"{s}{m}"]
                        ring.wait_full(dve, g, f"{s}{m}")
                        src = ring.bank(f"{s}{m}")[:, :].rearrange("p (b t) -> p b t", b=PAIR)
                        for n, f in enumerate((fa, fb)):
                            ins = nc.vector.tensor_tensor(
                                rot[s][:, 2 * m + n, :].rearrange("p (b t) -> p b t", b=PAIR), src, f, ALU.mult)
                        ins.then_inc(ring.reader(f"{s}{m}"), 1)

                def values(n):
                    yield from low(f"v{n}", v_hi[:, 2 * n:2 * n + 2, :].rearrange("p t d -> p (t d)"),
                                   v_lo[:, 2 * n:2 * n + 2, :].rearrange("p t d -> p (t d)"), SV / (SX * SW))

                for dt in range(DT):
                    yield from low(f"ctx{dt}", ct_hi[:, dt, :], ct_lo[:, dt, :], SX)
                yield from turn("k")
                yield from values(0)
                yield FILL["x0"] - 2
                dve.wait_ge(x_in[p], 16 * (i + 1))
                moments_of(dve, norm, x_tok[p])
                yield from values(1)
                yield FILL["x0"] - 1
                normalise(dve, norm, 0, rsqrt, g, x_tok[p])
                low_of_turned(dve, g, "k")
                for dt in range(DT):
                    yield from low(f"x{dt}", xt_hi[:, dt, :], xt_lo[:, dt, :], SX)
                yield from turn("q")
                yield FILL["q1"] + 3
                low_of_turned(dve, g, "q")
                for b in range(PAIR):
                    yield FILL[f"s{b}"]
                    ring.wait_full(dve, g, f"s{b}")
                    nc.vector.tensor_tensor(sc_f[:, b, :, :].rearrange("p k q -> p (k q)"), ring.bank(f"s{b}")[:, :],
                                            const("decay"), ALU.mult).then_inc(ring.reader(f"s{b}"), 1)
                for b in range(PAIR):
                    yield FILL[f"s{b}"] + 2
                    dve.wait_ge(hi_done.sem, hi_done.at(g, f"s{b}"))
                    nc.vector.tensor_tensor(sc_lo[:, b, :, :], sc_f[:, b, :, :], sc_hi[:, b, :, :], ALU.subtract) \
                      .then_inc(lo_done.sem, 1)
                for b in range(PAIR):
                    yield FILL[f"o{b}"]
                    ring.wait_full(dve, g, f"o{b}")
                    xs = x_tok[p][:, 2 * b:2 * b + 2, :].rearrange("p t d -> p (t d)")
                    nc.vector.scalar_tensor_tensor(out=xs, in0=ring.bank(f"o{b}")[:, :], scalar=step_of[:, 0:1], in1=xs,
                                                   op0=ALU.mult, op1=ALU.add).then_inc(ring.reader(f"o{b}"), 1)
                yield FILL["o1"] + 1
                for b in range(PAIR):
                    ring.wait_read(dve, g, f"o{b}")
                moments_of(dve, norm, x_tok[p])
                yield FILL["o1"] + 2
                normalise(dve, norm, 1, rsqrt, g, x_tok[p])
                for dt in range(DT):
                    yield from low(f"f{dt}", xf_hi[p][:, dt, :], xf_lo[p][:, dt, :], SX)
                yield FILL["logits"]
                ring.wait_full(dve, g, "logits")
                nc.vector.tensor_scalar(logit_t[:, :], ring.bank("logits")[0:EXPERTS, :], -1 / (SX * SW), 88.0,
                                        ALU.mult, ALU.min).then_inc(ring.reader("logits"), 1)
                for n, _ in enumerate(router(dve, g)):
                    yield FILL["logits_t"] + 1 + n
                yield FILL["comb_t"]
                low_of_bank(dve, ring, hi_done, g, "comb_t", "comb", comb_t[p][0:EXPERTS, :],
                            comb_t[p][EXPERTS:2 * EXPERTS, :], 1.0, rows=slice(0, EXPERTS))

            def low_of_turned(dve, g, s):
                dve.wait_ge(hi_done.sem, hi_done.at(g, s))
                nc.vector.tensor_tensor(rot_lo[s][:, :, :], rot[s][:, 0:2, :], rot_hi[s][:, :, :], ALU.subtract) \
                  .then_inc(lo_done.sem, 1)

            def router(dve, g):
                V = nc.vector

                def done(ins):
                    dve.drain()

                yield
                ring.wait_read(dve, g, "logits_t")
                done(V.tensor_scalar(expo[:, :, :], expo[:, :, :], 1.0, None, ALU.add))
                done(V.reciprocal(score[:, :, :], expo[:, :, :]))
                done(V.tensor_tensor(biased[:, :, :], score[:, :, :],
                                     bias_e[:, :].unsqueeze(1).to_broadcast([P, TT, EXPERTS]), ALU.add))
                yield
                four = biased[:, :, :].rearrange("p t (g f) -> p (t g) f", f=4)
                V.tensor_tensor(pair_hi[:, :, :], four[:, :, 0:2], four[:, :, 2:4], ALU.max)
                done(V.tensor_tensor(pair_lo[:, :, :], four[:, :, 0:2], four[:, :, 2:4], ALU.min))
                V.tensor_tensor(best[:, 0, :], pair_hi[:, :, 0], pair_hi[:, :, 1], ALU.max)
                V.tensor_tensor(best[:, 1, :], pair_hi[:, :, 0], pair_hi[:, :, 1], ALU.min)
                done(V.tensor_tensor(best[:, 2, :], pair_lo[:, :, 0], pair_lo[:, :, 1], ALU.max))
                done(V.tensor_tensor(best[:, 1, :], best[:, 1, :], best[:, 2, :], ALU.max))
                done(V.tensor_tensor(g_pad[:, :, 0:EXPERT_GROUPS], best[:, 0, :].rearrange("p (t g) -> p t g", t=TT),
                                     best[:, 1, :].rearrange("p (t g) -> p t g", t=TT), ALU.add))
                yield
                for tt in range(TT):
                    ins = V.max(top8[:, tt, :], g_pad[:, tt, :])
                done(ins)
                for tt in range(TT):
                    ins = V.match_replace(g_out[:, tt, :], top8[:, tt, :], g_pad[:, tt, :], -BIG)
                done(ins)
                yield
                done(V.tensor_scalar(g_mask[:, :, :], g_out[:, :, 0:EXPERT_GROUPS], -BIG, None, ALU.is_equal))
                for tt in range(TT):
                    ins = V.tensor_tensor(e_pad[:, tt, 0:EXPERTS].rearrange("p (g f) -> p g f", f=4),
                                          biased[:, tt, :].rearrange("p (g f) -> p g f", f=4),
                                          g_mask[:, tt, :].unsqueeze(2).to_broadcast([P, EXPERT_GROUPS, 4]), ALU.mult)
                done(ins)
                yield
                for tt in range(TT):
                    ins = V.max(top8[:, tt, :], e_pad[:, tt, :])
                done(ins)
                for tt in range(TT):
                    ins = V.match_replace(e_out[:, tt, :], top8[:, tt, :], e_pad[:, tt, :], -BIG)
                done(ins)
                yield
                done(V.scalar_tensor_tensor(out=chosen[:, :, :], in0=e_out[:, :, 0:EXPERTS], scalar=-BIG,
                                            in1=score[:, :, :], op0=ALU.is_equal, op1=ALU.mult))
                done(V.tensor_reduce(total[:, :], chosen[:, :, :], AX_X, ALU.add))
                done(V.tensor_scalar(total[:, :], total[:, :], 1e-20, None, ALU.add))
                done(V.reciprocal(total[:, :], total[:, :]))
                V.scalar_tensor_tensor(out=combine[:, :, :], in0=chosen[:, :, :], scalar=ROUTED_SCALE,
                                            in1=total[:, :].unsqueeze(2).to_broadcast([P, TT, EXPERTS]),
                                            op0=ALU.mult, op1=ALU.mult).then_inc(combined.sem, 1)

            def attend_pool(pool, i, j):
                g = 2 * i + j

                def power(k):
                    pool.wait_ge(norm.sem, norm.at(g, f"var{k}"))
                    nc.gpsimd.tensor_tensor(rstd[:, :], var_eps[:, :], minus_half[:, :], ALU.pow) \
                      .then_inc(rsqrt.sem, 1)

                def turn(s):
                    for m in range(2):
                        ring.wait_read(pool, g, f"{s}{m}")
                    nc.gpsimd.tensor_tensor(rot[s][:, 0, :], rot[s][:, 0, :], rot[s][:, 2, :], ALU.subtract)
                    nc.gpsimd.tensor_tensor(rot[s][:, 1, :], rot[s][:, 1, :], rot[s][:, 3, :], ALU.add) \
                      .then_inc(turned.sem, 1)

                yield FILL["k1"] + 1
                turn("k")
                yield FILL["x0"] - 2
                power(0)
                yield FILL["q1"] + 1
                turn("q")
                yield FILL["o1"] + 1
                power(1)

            def experts_pe(pe, i, j):
                p, g = j, 2 * i + j

                def up(e):
                    wait(pe, relu_done.sem, previous(relu_done, g, e - 2))
                    product(pe, hbank[e % 2][:, :],
                            [(weight(w_hi, "up", (e * DT + dt) * P, P), weight(w_lo, "up", (e * DT + dt) * P, P),
                              xf_hi[p][:, dt, :], xf_lo[p][:, dt, :]) for dt in range(DT)]).then_inc(up_done.sem, 1)

                def spread(e):
                    wait(pe, gated_done.sem, previous(gated_done, g, e - 1))
                    pe.matmul(cbank[:, :], pick16[0:96, e:e + 1].to_broadcast([96, P]), comb_t[p][:, :],
                              start=True, stop=True).then_inc(cb_done.sem, 1)

                def down(e):
                    pe.wait_ge(hid_lo_done.sem, hid_lo_done.at(g, e))
                    if e == 0:
                        wait(pe, x_done.sem, previous(x_done, g, -1))
                    for tt in range(TT):
                        hi, lo = (h[:, e % 3, tt * P:(tt + 1) * P] for h in (hid_hi, hid_lo))
                        for n, (a, b) in enumerate(parts3(hi, lo, weight(w_hi, "down", e * D, D),
                                                          weight(w_lo, "down", e * D, D))):
                            mm = pe.matmul(acc[tt // 2][:, (tt % 2) * D:(tt % 2 + 1) * D], a, b,
                                           start=e == 0 and n == 0 and tt % 2 == 0,
                                           stop=e == CHUNKS - 1 and n == 2, skip_group_check=True)
                    mm.then_inc(down_done.sem, 1)

                for dt in range(DT):
                    ring.wait_read(pe, g, f"f{dt}")
                for e in range(CHUNKS + 2):
                    if e < CHUNKS:
                        up(e)
                    if e == 0:
                        ring.wait_read(pe, g, "comb_t")
                    if e < EXPERTS:
                        spread(e)
                    if e >= 2:
                        down(e - 2)
                    yield

            def experts_act(act, i, j):
                g = 2 * i + j
                for e in range(CHUNKS + 1):
                    if e < CHUNKS:
                        act.wait_ge(up_done.sem, up_done.at(g, e))
                        wait(act, hid_done.sem, previous(hid_done, g, e - 2))
                        nc.scalar.activation(relu[:, e % 2, :], hbank[e % 2][:, :], ACT.Relu, scale=1 / (SX * SW)) \
                          .then_inc(relu_done.sem, 1)
                    if e >= 1:
                        act.wait_ge(hid_done.sem, hid_done.at(g, e - 1))
                        wait(act, down_done.sem, previous(down_done, g, e - 4))
                        nc.scalar.activation(hid_hi[:, (e - 1) % 3, :], hid[:, (e - 1) % 3, :], ACT.Copy) \
                          .then_inc(hid_hi_done.sem, 1)
                    yield

            def experts_dve(dve, i, j):
                p, g = j, 2 * i + j
                for e in range(CHUNKS + 1):
                    if e < EXPERTS:
                        dve.wait_ge(relu_done.sem, relu_done.at(g, e))
                        dve.wait_ge(cb_done.sem, cb_done.at(g, e))
                        wait(dve, hid_done.sem, previous(hid_done, g, e - 2))
                        nc.vector.tensor_tensor(gated[:, e % 2, :], relu[:, e % 2, :], cbank[:, :], ALU.mult) \
                          .then_inc(gated_done.sem, 1)
                    if e >= 1:
                        dve.wait_ge(hid_hi_done.sem, hid_hi_done.at(g, e - 1))
                        nc.vector.tensor_tensor(hid_lo[:, (e - 1) % 3, :], hid[:, (e - 1) % 3, :],
                                                hid_hi[:, (e - 1) % 3, :], ALU.subtract).then_inc(hid_lo_done.sem, 1)
                    yield
                dve.wait_ge(down_done.sem, down_done.at(g, CHUNKS - 1))
                for n in range(2):
                    xs = x_tok[p][:, 2 * n:2 * n + 2, :].rearrange("p t d -> p (t d)")
                    nc.vector.scalar_tensor_tensor(out=xs, in0=acc[n][:, :], scalar=step_of[:, 1:2], in1=xs,
                                                   op0=ALU.mult, op1=ALU.add).then_inc(x_done.sem, 1)
                yield

            def experts_pool(pool, i, j):
                g = 2 * i + j
                for e in range(CHUNKS):
                    if e < EXPERTS:
                        pool.wait_ge(gated_done.sem, gated_done.at(g, e))
                    else:
                        pool.wait_ge(relu_done.sem, relu_done.at(g, e))
                    wait(pool, hid_lo_done.sem, previous(hid_lo_done, g, e - 3))
                    by = gated if e < EXPERTS else relu
                    nc.gpsimd.tensor_tensor(hid[:, e % 3, :], relu[:, e % 2, :], by[:, e % 2, :], ALU.mult) \
                      .then_inc(hid_done.sem, 1)
                    yield

            def experts_sp(sp, i, j):
                g = 2 * i + j
                sp.wait_ge(x_done.sem, x_done.at(g, 1))
                sp.dma_start(x_mid[g], x_tok[j][:, :, :]).then_inc(x_out[j], 16)

            def both(eng, attend, experts):
                for _ in attend(eng, 0, 0):
                    pass
                with eng.Fori(0, GROUPS // 2 - 1) as i:
                    for j in range(2):
                        run(experts(eng, i, j), attend(eng, i + j, 1 - j))
                last = GROUPS // 2 - 1
                run(experts(eng, last, 0), attend(eng, last, 1))
                run(experts(eng, last, 1), iter(()))

            def run(main, side):
                never = 1000
                slot = next(side, never)
                for now, _ in enumerate(main):
                    while slot <= now:
                        slot = next(side, never)
                for _ in side:
                    pass

            @block.sync
            def _(sp):
                attend_sp(sp, 0, 0)
                attend_sp(sp, 0, 1)
                with sp.Fori(0, GROUPS // 2 - 1) as i:
                    for j in range(2):
                        experts_sp(sp, i, j)
                        attend_sp(sp, i + 1, j)
                for j in range(2):
                    experts_sp(sp, GROUPS // 2 - 1, j)
                for j in range(2):
                    sp.wait_ge(x_out[j], 16 * (GROUPS // 2))

            @block.tensor
            def _(pe):
                pe.wait_ge(preset, 1)
                both(pe, attend_pe, experts_pe)

            @block.scalar
            def _(act):
                both(act, attend_act, experts_act)

            @block.vector
            def _(dve):
                for p in range(2):
                    nc.vector.memset(comb_t[p][64:96, :], 0.0)
                nc.vector.memset(g_pad[:, :, EXPERT_GROUPS:], BIG)
                nc.vector.memset(e_pad[:, :, EXPERTS:], BIG).then_inc(preset, 1)
                dve.wait_ge(preset, 1)
                both(dve, attend_dve, experts_dve)

            @block.gpsimd
            def _(pool):
                for s in (norm, rsqrt, hi_done, lo_done, turned, combined, up_done, relu_done, cb_done, gated_done,
                          hid_done, hid_hi_done, hid_lo_done, down_done, x_done):
                    pool.sem_inc(s.sem, HEAD)
                for s in ring.read:
                    pool.sem_inc(s, HEAD)
                both(pool, attend_pool, experts_pool)

        with ExitStack() as second:
            x_tok = sb("x_tok", [P, TT, D], to=second)
            ctx_tok = sb("ctx_tok1", [P, TT, D], to=second)
            xn = sb("xn1", [P, TT, D], to=second)
            stats = sb("stats1", [P, TT, 6], to=second)
            moments = sb("moments1", [P, TT, 2], to=second)
            var_eps = sb("var_eps1", [P, TT], to=second)
            rstd = sb("rstd1", [P, TT], to=second)
            xt_hi, xt_lo = (sb(f"xt1_{n}", [P, DT, T], F16, second) for n in ("hi", "lo"))
            ct_hi, ct_lo = (sb(f"ct1_{n}", [P, DT, T], F16, second) for n in ("hi", "lo"))
            qk = sb("qk", [P, 4, T], to=second)
            qk_hi, qk_lo = (sb(f"qk_{n}", [P, 4, T], F16, second) for n in ("hi", "lo"))
            v_one = sb("v_one", [P, TT, HEADS, 2 * HD], to=second)
            q_stack, k_stack = (sb(f"{n}_stack", [P, HEADS, SEQ], F16, second) for n in "qk")
            row_max = sb("row_max", [P, 2, HEADS], to=second)
            max_hi, max_lo = (sb(f"max_{n}", [HEADS, SEQ], F16, second) for n in ("hi", "lo"))
            NPR = 3
            prob = sb("prob", [P, NPR, 2, SEQ], to=second)
            mixed = sb("mixed", [P, 2, 2 * SEQ], to=second)
            inverse = sb("inverse", [P, 2 * SEQ], to=second)
            att = sb("att", [P, 2, 2 * SEQ], to=second)
            att_hi, att_lo = (sb(f"att_{n}", [P, 4, SEQ], F16, second) for n in ("hi", "lo"))
            proj = sb("proj", [P, 2, D], to=second)
            xf_hi, xf_lo = (sb(f"xf1_{n}", [P, DT, T], F16, second) for n in ("hi", "lo"))
            relu, hid = mixed, att
            hid_hi, hid_lo = (t[:, :, :].rearrange("p (f a) q -> p f (a q)", f=2) for t in (att_hi, att_lo))
            drive = qk[:, 0:2, :].rearrange("p n t -> p (n t)")
            mem = qk[:, 2:4, :].rearrange("p n t -> p (n t)")
            leak = prob[:, 0:2, :, :].rearrange("p n k q -> p (n k q)")
            spikes = xn[:, :, :].rearrange("p t d -> p (t d)")

            acc, hbank, ubank = psum[0:2], psum[2:4], psum[4]
            heads = range(HEADS)
            STEP1 = ["ctx0", "ctx1", "x0", "x1", "q0", "q1", "k0", "k1", "v0", "v1"]
            for b in range(PAIR):
                STEP1 += [f"{b}max{h}" for h in heads] + [f"{b}turn"] + [f"{b}exp{h}" for h in heads]
                STEP1 += [f"{b}den0", f"{b}den1", f"{b}wo"]
            STEP1 += ["f0", "f1"]
            ring = Banks(psum[5:8], sem("b_bank_full"), [sem(f"b_bank_read{b}") for b in range(3)], STEP1)
            x_in, ctx_in, x_out = sem("b_x_in"), sem("b_ctx_in"), sem("b_x_out")
            norm = Signal(sem("b_norm"), [f"{n}{k}" for k in range(2) for n in ("var", "xn")])
            rsqrt = Signal(sem("b_rsqrt"), ["0", "1"])
            hi_done = Signal(sem("b_hi_done"), ["ctx0", "ctx1", "x0", "x1", "q0", "q1", "k0", "k1"]
                             + [f"{b}{e}" for b in range(PAIR) for e in ("max", "att0", "att1")] + ["f0", "f1"])
            lo_done = Signal(sem("b_lo_done"), ["q0", "q1", "k0", "k1"] + [f"{b}att{n}" for b in range(PAIR) for n in range(2)])
            values = Signal(sem("b_values"), range(TT))
            stacked = sem("b_stacked")
            max_stacked = sem("b_max_stacked")
            STACK_DMAS = 12
            mix_full = Signal(sem("b_mix_full"), [f"{b}{n}" for b in range(PAIR) for n in range(2)])
            mix_read = Signal(sem("b_mix_read"), [f"{b}{n}" for b in range(PAIR) for n in range(2)])
            mixing = Signal(sem("b_mixing"), [f"{b}head{h}" for b in range(PAIR) for h in heads])
            inverted = Signal(sem("b_inverted"), [f"{b}{n}" for b in range(PAIR) for n in range(2)])
            att_done = Signal(sem("b_att_done"), [f"{b}{n}" for b in range(PAIR) for n in range(2)])
            x_mixed = Signal(sem("b_x_mixed"), range(PAIR))
            up_done = Signal(sem("b_up_done"), range(FC))
            relu_done = Signal(sem("b_relu_done"), range(FC))
            hid_done = Signal(sem("b_hid_done"), range(FC))
            hid_hi_done = Signal(sem("b_hid_hi_done"), range(FC))
            hid_lo_done = Signal(sem("b_hid_lo_done"), range(FC))
            down_done = Signal(sem("b_down_done"), range(FC))
            driven = Signal(sem("b_driven"), range(2))
            fire = Signal(sem("b_fire"), [f"{n}{k}" for k in range(2, STEPS + 1) for n in ("leak", "mem")] + ["x"])
            preset = sem("b_preset")

            block = second.enter_context(nc.Block())

            @block.sync
            def _(sp):
                sp.dma_start(x_tok[:, :, :], x_mid[0]).then_inc(x_in, 16)
                sp.dma_start(ctx_tok[:, :, :], ctx[0]).then_inc(ctx_in, 16)
                sp.wait_ge(preset, 1)

                def group(g, more):
                    for b in range(PAIR):
                        sp.wait_ge(lo_done.sem, lo_done.at(g, "k1"))
                        if b == 0:
                            if more is not None:
                                sp.wait_ge(ring.full, ring.full_at(g - 1, f"1exp{HEADS - 1}"))
                        else:
                            ring.wait_full(sp, g, f"0exp{HEADS - 1}")
                        for stack, first_tile, roles in ((q_stack, 0, (qk_hi, qk_lo, qk_hi)), (k_stack, 2, (qk_hi, qk_hi, qk_lo))):
                            for r, part in enumerate(roles):
                                for ct in range(2):
                                    sp.dma_start(stack[r * HD:(r + 1) * HD, ct * 8:(ct + 1) * 8, :],
                                                 part[:, first_tile + ct, b * SEQ:(b + 1) * SEQ]).then_inc(stacked, 16)
                        ring.wait_read(sp, g, f"{b}turn")
                        sp.dma_start(q_stack[96:97, :, :], max_hi[:, :]).then_inc(max_stacked, 16)
                        sp.dma_start(q_stack[97:98, :, :], max_lo[:, :]).then_inc(max_stacked, 16)
                        if b == 0 and more is not False:
                            sp.dma_start(ctx_tok[:, :, :], ctx[g + 1]).then_inc(ctx_in, 16)
                    sp.wait_ge(fire.sem, fire.at(g, "x"))
                    sp.dma_start(out[g], x_tok[:, :, :]).then_inc(x_out, 16)
                    if more is not False:
                        sp.wait_ge(x_out, 16 * (g + 1))
                        sp.dma_start(x_tok[:, :, :], x_mid[g + 1]).then_inc(x_in, 16)

                group(0, None)
                with sp.Fori(1, GROUPS - 1) as g:
                    group(g, True)
                group(GROUPS - 1, False)
                sp.wait_ge(x_out, 16 * GROUPS)

            @block.tensor
            def _(pe):
                pe.wait_ge(preset, 1)
                with pe.Fori(0, GROUPS) as g:
                    def fill(step):
                        ring.wait_free(pe, g, step)
                        return ring.bank(step)

                    pe.wait_ge(ctx_in, 16 * (g + 1))
                    for dt in range(DT):
                        transposes(pe, fill(f"ctx{dt}"), ctx_tok, dt).then_inc(ring.full, 1)
                    pe.wait_ge(norm.sem, norm.at(g, "xn0"))
                    for dt in range(DT):
                        transposes(pe, fill(f"x{dt}"), xn, dt).then_inc(ring.full, 1)
                    for s, (a_hi, a_lo), src in (("q", (xt_hi, xt_lo), "x"), ("k", (ct_hi, ct_lo), "ctx")):
                        for m in range(2):
                            b = fill(f"{s}{m}")
                            for dt in range(DT):
                                ring.wait_read(pe, g, f"{src}{dt}")
                            product(pe, b[:, :], [(weight(w_hi, f"w{s}1", dt * D + m * P, P),
                                                   weight(w_lo, f"w{s}1", dt * D + m * P, P),
                                                   a_hi[:, dt, :], a_lo[:, dt, :]) for dt in range(DT)]) \
                                .then_inc(ring.full, 1)
                    for n in range(2):
                        b = fill(f"v{n}")
                        for half in range(2):
                            tt = 2 * n + half
                            mm = product(pe, b[:, half * D:(half + 1) * D],
                                         [(ct_hi[:, dt, tt * P:(tt + 1) * P], ct_lo[:, dt, tt * P:(tt + 1) * P],
                                           weight(w_hi, "wv1", dt * D, D), weight(w_lo, "wv1", dt * D, D))
                                          for dt in range(DT)])
                        mm.then_inc(ring.full, 1)
                    for b in range(PAIR):
                        pe.wait_ge(stacked, HEAD + (g * PAIR + b + 1) * (16 * STACK_DMAS))
                        for h in heads:
                            bank = fill(f"{b}max{h}")
                            for qt in range(2):
                                mm = pe.matmul(bank[:, qt * SEQ:(qt + 1) * SEQ], q_stack[0:96, h, qt * P:(qt + 1) * P],
                                               k_stack[0:96, h, :], start=True, stop=True)
                            mm.then_inc(ring.full, 1)
                        bank = fill(f"{b}turn")
                        ring.wait_read(pe, g, f"{b}max{HEADS - 1}")
                        ring.wait_read(pe, g, f"{b}max{HEADS - 2}")
                        ring.wait_read(pe, g, f"{b}max{HEADS - 3}")
                        for qt in range(2):
                            mm = pe.transpose(bank[0:HEADS, qt * P:(qt + 1) * P], row_max[:, qt, :], ident)
                        mm.then_inc(ring.full, 1)
                        pe.wait_ge(max_stacked, HEAD + (g * PAIR + b + 1) * 32)

                        def scores(h):
                            bank = fill(f"{b}exp{h}")
                            for kt in range(2):
                                mm = pe.matmul(bank[:, kt * SEQ:(kt + 1) * SEQ], k_stack[0:98, h, kt * P:(kt + 1) * P],
                                               q_stack[0:98, h, :], start=True, stop=True)
                            mm.then_inc(ring.full, 1)

                        def mix(h):
                            n, half, c = h // 8, (h // 4) % 2, h % 4
                            if h == 0:
                                pe.wait_ge(values.sem, values.at(g, 2 * b + 1))
                            if h % 8 == 0:
                                wait(pe, mix_read.sem, mix_read.at(g, f"{b}{n}") - 1)
                            ring.wait_read(pe, g, f"{b}exp{h}")
                            for kt in range(2):
                                mm = pe.matmul(ubank[32 * c:32 * c + 32, half * SEQ:(half + 1) * SEQ],
                                               v_one[:, 2 * b + kt, h, :], prob[:, h % NPR, kt, :],
                                               start=kt == 0, stop=kt == 1, tile_position=(0, 32 * c))
                            mm.then_inc(mixing.sem, 1)

                        def denominators(n):
                            bank = fill(f"{b}den{n}")
                            pe.wait_ge(mix_read.sem, mix_read.at(g, f"{b}{n}"))
                            pe.matmul(bank[:, :], const("den"), mixed[:, n, :], start=True, stop=True) \
                                .then_inc(ring.full, 1)

                        for h in range(HEADS + 2):
                            if h < HEADS:
                                scores(h)
                            if h >= 2:
                                mix(h - 2)
                        denominators(0)
                        denominators(1)
                        bank = fill(f"{b}wo")
                        pe.wait_ge(lo_done.sem, lo_done.at(g, f"{b}att1"))
                        for qt in range(2):
                            mm = product(pe, bank[:, qt * D:(qt + 1) * D],
                                         [(att_hi[:, n, qt * P:(qt + 1) * P], att_lo[:, n, qt * P:(qt + 1) * P],
                                           weight(w_hi, "wo", n * D, D), weight(w_lo, "wo", n * D, D)) for n in range(4)])
                        mm.then_inc(ring.full, 1)
                    pe.wait_ge(norm.sem, norm.at(g, "xn1"))
                    for dt in range(DT):
                        transposes(pe, fill(f"f{dt}"), xn, dt).then_inc(ring.full, 1)
                    for dt in range(DT):
                        ring.wait_read(pe, g, f"f{dt}")

                    def up(f):
                        if f >= 2:
                            pe.wait_ge(relu_done.sem, relu_done.at(g, f - 2))
                        product(pe, hbank[f % 2][:, :],
                                [(weight(w_hi, "fc", (f * DT + dt) * P, P), weight(w_lo, "fc", (f * DT + dt) * P, P),
                                  xf_hi[:, dt, :], xf_lo[:, dt, :]) for dt in range(DT)]).then_inc(up_done.sem, 1)

                    def down(f):
                        pe.wait_ge(hid_lo_done.sem, hid_lo_done.at(g, f))
                        for tt in range(TT):
                            hi, lo = (h[:, f % 2, tt * P:(tt + 1) * P] for h in (hid_hi, hid_lo))
                            for n, (a, b) in enumerate(parts3(hi, lo, weight(w_hi, "proj", f * D, D),
                                                              weight(w_lo, "proj", f * D, D))):
                                mm = pe.matmul(acc[tt // 2][:, (tt % 2) * D:(tt % 2 + 1) * D], a, b,
                                               start=f == 0 and n == 0 and tt % 2 == 0,
                                               stop=f == FC - 1 and n == 2, skip_group_check=True)
                        mm.then_inc(down_done.sem, 1)

                    for f in range(FC + 2):
                        if f < FC:
                            up(f)
                        if f >= 2:
                            down(f - 2)

            @block.scalar
            def _(act):
                with act.Fori(0, GROUPS) as g:
                    for src, hi in (("ctx", ct_hi), ("x", xt_hi)):
                        for dt in range(DT):
                            ring.wait_full(act, g, f"{src}{dt}")
                            nc.scalar.activation(hi[:, dt, :], ring.bank(f"{src}{dt}")[:, :], ACT.Copy, scale=SX) \
                              .then_inc(hi_done.sem, 1)
                    for n, s in enumerate(("q0", "q1", "k0", "k1")):
                        ring.wait_full(act, g, s)
                        nc.scalar.activation(qk[:, n, :], ring.bank(s)[:, :], ACT.Identity, bias=bias_qk[:, n:n + 1],
                                             scale=1 / (SX * SW)).then_inc(ring.reader(s), 1)
                        ring.wait_read(act, g, s)
                        if n == 0:
                            wait(act, stacked, HEAD + g * PAIR * (16 * STACK_DMAS))
                        nc.scalar.activation(qk_hi[:, n, :], qk[:, n, :], ACT.Copy).then_inc(hi_done.sem, 1)
                    for b in range(PAIR):
                        ring.wait_full(act, g, f"{b}turn")
                        wait(act, max_stacked, HEAD + (g * PAIR + b) * 32)
                        nc.scalar.activation(max_hi[:, :], ring.bank(f"{b}turn")[0:HEADS, 0:SEQ], ACT.Copy,
                                             scale=-1 / SM).then_inc(hi_done.sem, 1)

                        def evacuate(n):
                            act.wait_ge(mixing.sem, mixing.at(g, f"{b}head{8 * n + 7}"))
                            nc.scalar.activation(mixed[:, n, :], ubank[:, :], ACT.Copy).then_inc(mix_read.sem, 1)

                        for h in heads:
                            ring.wait_full(act, g, f"{b}exp{h}")
                            wait(act, mixing.sem, mixing.at(g, f"{b}head{h}") - NPR)
                            nc.scalar.activation(prob[:, h % NPR, :, :], ring.bank(f"{b}exp{h}")[:, :], ACT.Exp,
                                                 scale=float(HD) ** -0.5).then_inc(ring.reader(f"{b}exp{h}"), 1)
                            if h == 9:
                                evacuate(0)
                        evacuate(1)
                        for n in range(2):
                            act.wait_ge(att_done.sem, att_done.at(g, f"{b}{n}"))
                            nc.scalar.activation(att_hi[:, 2 * n:2 * n + 2, :], att[:, n, :], ACT.Copy) \
                              .then_inc(hi_done.sem, 1)
                    for dt in range(DT):
                        ring.wait_full(act, g, f"f{dt}")
                        nc.scalar.activation(xf_hi[:, dt, :], ring.bank(f"f{dt}")[:, :], ACT.Copy, scale=SX) \
                          .then_inc(hi_done.sem, 1)
                    for f in range(FC + 1):
                        if f < FC:
                            act.wait_ge(up_done.sem, up_done.at(g, f))
                            if f >= 2:
                                act.wait_ge(hid_done.sem, hid_done.at(g, f - 2))
                            nc.scalar.activation(relu[:, f % 2, :], hbank[f % 2][:, :], ACT.Relu,
                                                 scale=SF ** 0.5 / (SX * SW)).then_inc(relu_done.sem, 1)
                        if f >= 1:
                            act.wait_ge(hid_done.sem, hid_done.at(g, f - 1))
                            if f >= 3:
                                act.wait_ge(down_done.sem, down_done.at(g, f - 3))
                            nc.scalar.activation(hid_hi[:, (f - 1) % 2, :], hid[:, (f - 1) % 2, :], ACT.Copy) \
                              .then_inc(hid_hi_done.sem, 1)
                    act.wait_ge(down_done.sem, down_done.at(g, FC - 1))
                    for n in range(2):
                        nc.scalar.activation(drive[:, n * 2 * D:(n + 1) * 2 * D], acc[n][:, :], ACT.Copy,
                                             scale=1 / (SW * SF)).then_inc(driven.sem, 1)

            @block.vector
            def _(dve):
                nc.vector.memset(q_stack[:, :, :].bitcast(F32), 0.0).then_inc(preset, 1)
                nc.vector.memset(k_stack[:, :, :].bitcast(F32), 0.0).then_inc(preset, 1)
                nc.vector.memset(v_one[:, :, :, :], 1.0).then_inc(preset, 1)
                dve.wait_ge(preset, 3)
                nc.vector.memset(k_stack[96:98, :, :], SM).then_inc(preset, 1)
                V = nc.vector
                with dve.Fori(0, GROUPS) as g:
                    for dt in range(DT):
                        low_of_bank(dve, ring, hi_done, g, f"ctx{dt}", f"ctx{dt}", ct_hi[:, dt, :], ct_lo[:, dt, :], SX)
                    dve.wait_ge(x_in, 16 * (g + 1))
                    moments_of(dve, norm, x_tok)
                    normalise(dve, norm, 0, rsqrt, g, x_tok)
                    for dt in range(DT):
                        low_of_bank(dve, ring, hi_done, g, f"x{dt}", f"x{dt}", xt_hi[:, dt, :], xt_lo[:, dt, :], SX)
                    for n, s in enumerate(("q0", "q1", "k0", "k1")):
                        dve.wait_ge(hi_done.sem, hi_done.at(g, s))
                        V.tensor_tensor(qk_lo[:, n, :], qk[:, n, :], qk_hi[:, n, :], ALU.subtract).then_inc(lo_done.sem, 1)
                    for n in range(2):
                        ring.wait_full(dve, g, f"v{n}")
                        for half in range(2):
                            ins = V.scalar_tensor_tensor(
                                out=v_one[:, 2 * n + half, :, 0:HD],
                                in0=ring.bank(f"v{n}")[:, half * D:(half + 1) * D].rearrange("p (h d) -> p h d", h=HEADS),
                                scalar=1 / (SX * SW), in1=bias_v[:, :].rearrange("p (h d) -> p h d", h=HEADS),
                                op0=ALU.mult, op1=ALU.add).then_inc(values.sem, 1)
                        V.engine_nop().then_inc(ring.reader(f"v{n}"), 1)
                    for b in range(PAIR):
                        for h in heads:
                            ring.wait_full(dve, g, f"{b}max{h}")
                            V.tensor_reduce(row_max[:, :, h], ring.bank(f"{b}max{h}")[:, :].rearrange("p (q k) -> p q k", q=2),
                                            AX_X, ALU.max).then_inc(ring.reader(f"{b}max{h}"), 1)
                        low_of_bank(dve, ring, hi_done, g, f"{b}turn", f"{b}max", max_hi[:, :], max_lo[:, :], -1 / SM,
                                    cols=slice(0, SEQ), rows=slice(0, HEADS))
                        for n in range(2):
                            ring.wait_full(dve, g, f"{b}den{n}")
                            V.reciprocal(inverse[:, :], ring.bank(f"{b}den{n}")[:, :]).then_inc(ring.reader(f"{b}den{n}"), 1)
                            ring.wait_read(dve, g, f"{b}den{n}")
                            V.tensor_tensor(att[:, n, :], mixed[:, n, :], inverse[:, :], ALU.mult).then_inc(att_done.sem, 1)
                            dve.wait_ge(hi_done.sem, hi_done.at(g, f"{b}att{n}"))
                            V.tensor_tensor(att_lo[:, 2 * n:2 * n + 2, :].rearrange("p n q -> p (n q)"), att[:, n, :],
                                            att_hi[:, 2 * n:2 * n + 2, :].rearrange("p n q -> p (n q)"), ALU.subtract) \
                             .then_inc(lo_done.sem, 1)
                        ring.wait_full(dve, g, f"{b}wo")
                        V.scalar_tensor_tensor(out=proj[:, :, :], in0=ring.bank(f"{b}wo")[:, :].rearrange("p (q d) -> p q d", q=2),
                                               scalar=1 / SW, in1=bias_o[:, :].unsqueeze(1).to_broadcast([P, 2, D]),
                                               op0=ALU.mult, op1=ALU.add).then_inc(ring.reader(f"{b}wo"), 1)
                        ring.wait_read(dve, g, f"{b}wo")
                        xs = x_tok[:, 2 * b:2 * b + 2, :]
                        V.scalar_tensor_tensor(out=xs, in0=proj[:, :, :], scalar=step_of[:, 2:3], in1=xs,
                                               op0=ALU.mult, op1=ALU.add).then_inc(x_mixed.sem, 1)
                        dve.wait_ge(x_mixed.sem, x_mixed.at(g, b))
                    moments_of(dve, norm, x_tok)
                    normalise(dve, norm, 1, rsqrt, g, x_tok)
                    for dt in range(DT):
                        low_of_bank(dve, ring, hi_done, g, f"f{dt}", f"f{dt}", xf_hi[:, dt, :], xf_lo[:, dt, :], SX)
                    for f in range(FC):
                        dve.wait_ge(hid_hi_done.sem, hid_hi_done.at(g, f))
                        V.tensor_tensor(hid_lo[:, f % 2, :], hid[:, f % 2, :], hid_hi[:, f % 2, :], ALU.subtract) \
                         .then_inc(hid_lo_done.sem, 1)
                    dve.wait_ge(driven.sem, driven.at(g, 1))
                    V.tensor_scalar(spikes[:, :], drive[:, :], THRESHOLD, None, ALU.is_gt)
                    before = drive
                    for k in range(2, STEPS + 1):
                        V.scalar_tensor_tensor(out=leak[:, :], in0=before[:, :], scalar=BETA, in1=drive[:, :],
                                               op0=ALU.mult, op1=ALU.add).then_inc(fire.sem, 1)
                        dve.wait_ge(fire.sem, fire.at(g, f"leak{k}"))
                        V.scalar_tensor_tensor(out=mem[:, :], in0=before[:, :], scalar=THRESHOLD, in1=leak[:, :],
                                               op0=ALU.is_gt, op1=ALU.subtract, reverse1=True).then_inc(fire.sem, 1)
                        dve.wait_ge(fire.sem, fire.at(g, f"mem{k}"))
                        V.scalar_tensor_tensor(out=spikes[:, :], in0=mem[:, :], scalar=THRESHOLD, in1=spikes[:, :],
                                               op0=ALU.is_gt, op1=ALU.add)
                        before = mem
                    xs = x_tok[:, :, :].rearrange("p t d -> p (t d)")
                    V.drain()
                    V.scalar_tensor_tensor(out=xs, in0=spikes[:, :], scalar=step_of[:, 3:4], in1=xs,
                                           op0=ALU.mult, op1=ALU.add).then_inc(fire.sem, 1)

            @block.gpsimd
            def _(pool):
                for s in (norm, rsqrt, hi_done, lo_done, values, mix_full, mix_read, mixing, inverted, att_done,
                          x_mixed, up_done, relu_done, hid_done, hid_hi_done, hid_lo_done, down_done, driven, fire):
                    pool.sem_inc(s.sem, HEAD)
                for s in (*ring.read, stacked, max_stacked):
                    pool.sem_inc(s, HEAD)
                with pool.Fori(0, GROUPS) as g:
                    def power(k):
                        pool.wait_ge(norm.sem, norm.at(g, f"var{k}"))
                        nc.gpsimd.tensor_tensor(rstd[:, :], var_eps[:, :], minus_half[:, :], ALU.pow) \
                          .then_inc(rsqrt.sem, 1)

                    power(0)
                    power(1)
                    for f in range(FC):
                        pool.wait_ge(relu_done.sem, relu_done.at(g, f))
                        if f >= 2:
                            pool.wait_ge(hid_lo_done.sem, hid_lo_done.at(g, f - 2))
                        nc.gpsimd.tensor_tensor(hid[:, f % 2, :], relu[:, f % 2, :], relu[:, f % 2, :], ALU.mult) \
                          .then_inc(hid_done.sem, 1)


_INS = ("x", "ctx", "gates", "weights", "consts", "ebias", "bqk", "bv", "bo")


def kernel(**inputs):
    import concourse.bacc as _bacc
    from concourse.bass_utils import run_bass_kernel_spmd as _run

    a = {k: np.asarray(v) for k, v in inputs.items()}

    def tokens(v):
        return np.ascontiguousarray(v.reshape(GROUPS, TT, P, D).transpose(0, 2, 1, 3))

    def rows(w, cols=None):
        w = w if cols is None else w[:, cols]
        return w.reshape(DT, P, -1).transpose(1, 0, 2).reshape(P, -1)

    def up(w):
        return w.reshape(-1, P, DT, P).transpose(3, 0, 2, 1).reshape(P, -1)

    def down(w):
        return w.reshape(D, -1, P).transpose(2, 1, 0).reshape(P, -1)

    halves = np.concatenate([np.arange(0, D, 2), np.arange(1, D, 2)])
    by_place = np.arange(D).reshape(2, HEADS // 2, HD).transpose(0, 2, 1).reshape(D)
    wo = a["L1_xattn_wo"].reshape(4, 4, HD, D).transpose(1, 2, 0, 3)
    wo_rows = np.zeros((4, 2 * HD, 4, D), np.float32)
    wo_rows[:, :HD] = wo
    packed = [rows(a["L0_xattn_Wq"], halves), rows(a["L0_xattn_Wk"], halves), rows(a["L0_xattn_Wv"]),
              rows(a["L0_ffn_gate_w"].T),
              up(np.concatenate([a["L0_ffn_up_w"].reshape(EXPERTS * P, D), a["L0_ffn_shared_up_w"]])),
              np.concatenate([a["L0_ffn_down_w"].transpose(2, 0, 1).reshape(P, -1), down(a["L0_ffn_shared_down_w"])], axis=1),
              rows(a["L1_xattn_wq"], by_place), rows(a["L1_xattn_wk"], by_place), rows(a["L1_xattn_wv"]),
              wo_rows.reshape(P, 4 * D), up(a["L1_ffn_W_fc"]), down(a["L1_ffn_W_proj"])]
    used = sum(w.shape[1] for w in packed)
    packed.append(np.zeros((P, WCOLS - used), np.float32))
    bqk = np.stack([a[n][by_place].reshape(2, P) for n in ("L1_xattn_bq", "L1_xattn_bk")]).reshape(4, P).T
    arrays = {
        "x": tokens(a["x"]), "ctx": tokens(a["ctx_1024"]),
        "gates": np.stack([a["g_xattn"], a["g_ffn"]], axis=1).reshape(4),
        "weights": np.concatenate(packed, axis=1), "consts": constants(),
        "ebias": a["L0_ffn_e_bias"], "bqk": bqk, "bv": a["L1_xattn_bv"], "bo": a["L1_xattn_bo"],
    }
    arrays = {f"in_{k}": np.ascontiguousarray(v) for k, v in arrays.items()}
    nc = _bacc.Bacc("TRN2", target_bir_lowering=False, num_devices=1)
    aps = [nc.dram_tensor(k, v.shape, F32, kind="ExternalInput").ap() for k, v in arrays.items()]
    x_mid = nc.dram_tensor("x_mid", (GROUPS, P, TT, D), F32, kind="Internal").ap()
    out = nc.dram_tensor("out_x", (GROUPS, P, TT, D), F32, kind="ExternalOutput").ap()
    build(nc, *aps, x_mid, out)
    r = _run(nc, [arrays], core_ids=[0])
    got = r.results[0]["out_x"]
    return got.reshape(GROUPS, P, TT, D).transpose(0, 2, 1, 3).reshape(NB, SEQ, D)
```

```python
from contextlib import ExitStack

import numpy as np

import concourse.bass as bass
from concourse import mybir

F32 = mybir.dt.float32
F16 = mybir.dt.float16
ALU = mybir.AluOpType
ACT = mybir.ActivationFunctionType
AX_X = mybir.AxisListType.X

P = 128
NB, SEQ, D = 16, 256, 256
DT = D // P
PAIR = 2
T = PAIR * SEQ
TT = T // P
GROUPS = NB // PAIR
EXPERTS, SHARED = 32, 4
CHUNKS = EXPERTS + SHARED
FC = 8
TOP_GROUPS, TOP_K = 4, 6
EXPERT_GROUPS = 8
ROUTED_SCALE = 2.5
HEADS, HD = 16, 16
STEPS, BETA, THRESHOLD = 5, 0.9, 1.0
EPS = 1e-5

SX = 16.0
SW = 256.0
SR = 8.0
SV = 16.0
SM = 16.0
SF = 1.0 / 16.0
BIG = 1.0e30

WEIGHTS = {}


def pack(part, sizes):
    at = 0
    for name, n in sizes:
        WEIGHTS[name] = (part, at, n)
        at += n
    return at


STAGES = 3
_cols = (pack(0, (("wq0", DT * D), ("wk0", DT * D), ("wv0", DT * D), ("gate", DT * EXPERTS),
                  ("up", CHUNKS * DT * P), ("down", CHUNKS * D))),
         pack(1, (("wq1", DT * D), ("wk1", DT * D), ("wv1", DT * D), ("wo", 4 * D),
                  ("fc", FC * DT * P), ("proj", FC * D))))
ROUNDS = 7
PIECES1 = 6
STAGE = (-(-_cols[0] // (ROUNDS * STAGES)), -(-_cols[1] // PIECES1))
WCOLS = (STAGE[0] * ROUNDS * STAGES, STAGE[1] * PIECES1)

CONSTS = {}
CCOLS = 0
for _name, _n in (("ident", P), ("cq", SEQ), ("sq", SEQ), ("ck", SEQ), ("sk", SEQ),
                  ("decay", 2 * SEQ), ("den", P), ("pick", EXPERTS)):
    CONSTS[_name] = (CCOLS, _n)
    CCOLS += _n


HEAD = 4


class Signal:

    def __init__(self, sem, events):
        self.sem = sem
        self.events = list(events)

    def at(self, g, event):
        return HEAD + g * len(self.events) + self.events.index(event) + 1


def wait(eng, sem, value):
    if not isinstance(value, int) or value > 0:
        eng.wait_ge(sem, value)


class Banks:

    def __init__(self, banks, full, read, steps):
        self.banks, self.full, self.read, self.steps = banks, full, read, list(steps)

    def bank(self, step):
        return self.banks[self.steps.index(step) % len(self.banks)]

    def reader(self, step):
        return self.read[self.steps.index(step) % len(self.banks)]

    def full_at(self, g, step):
        return g * len(self.steps) + self.steps.index(step) + 1

    def read_at(self, g, step, done=1):
        k, n = self.steps.index(step), len(self.banks)
        return HEAD + g * len(range(k % n, len(self.steps), n)) + k // n + done

    def wait_free(self, eng, g, step):
        wait(eng, self.reader(step), self.read_at(g, step, 0))

    def wait_full(self, eng, g, step):
        eng.wait_ge(self.full, self.full_at(g, step))

    def wait_read(self, eng, g, step):
        eng.wait_ge(self.reader(step), self.read_at(g, step))


def constants():
    c = np.zeros((P, CCOLS), np.float32)

    def put(name, a):
        o, n = CONSTS[name]
        c[:a.shape[0], o:o + n] = a.reshape(a.shape[0], n)

    half = D // 2
    scale_vec = (np.arange(0, D, 2, dtype=np.float32) + np.float32(0.4 * D)) / np.float32(1.4 * D)
    pos = np.arange(SEQ, dtype=np.float32)
    scale = scale_vec[None, :] ** (pos / np.float32(512.0))[:, None]
    freqs = np.float32(1.0) / np.float32(10000.0) ** (np.arange(half, dtype=np.float32) / np.float32(half))
    angle = pos[:, None] * freqs[None, :]
    undo = np.float32(SR / (SX * SW))
    put("cq", (np.cos(angle) * scale * undo).T)
    put("sq", (np.sin(angle) * scale * undo).T)
    put("ck", (np.cos(angle) * (1.0 / scale) * undo).T)
    put("sk", (np.sin(angle) * (1.0 / scale) * undo).T)
    key = np.arange(P)[:, None, None] + P * np.arange(2)[None, :, None]
    gap = np.arange(SEQ)[None, None, :] - key
    put("decay", np.where(gap >= 0, np.float32(0.96875) ** gap.astype(np.float32), 0) / (SR * SR))
    put("ident", np.eye(P))
    den = np.zeros((P, P))
    den[32 * (np.arange(P) // 32) + HD, np.arange(P)] = 1
    put("den", den)
    pick = np.zeros((P, EXPERTS))
    pick[np.arange(64), np.arange(64) % 32] = 1
    put("pick", pick)
    return c


def build(nc, x, ctx, gates, weights0, weights1, consts, ebias, bqk, bv, bo, x_mid, den_mid, out):
    with ExitStack() as whole:
        sem = lambda name: whole.enter_context(nc.semaphore(name))
        psum = [whole.enter_context(nc.psum_tensor(f"bank{b}", [P, 512], F32)) for b in range(8)]

        def sb(name, shape, dt=F32, to=whole):
            return to.enter_context(nc.sbuf_tensor(name, shape, dt))

        w1_hi, w1_lo = (sb(f"w1_{n}", [P, WCOLS[1]], F16) for n in ("hi", "lo"))
        table = sb("table", [P, CCOLS])
        pick16 = sb("pick16", [P, EXPERTS], F16)
        minus_half = sb("minus_half", [P, TT])
        gate_in = sb("gate_in", [P, 4])
        tanh_g = sb("tanh_g", [P, 4])
        step_of = sb("step_of", [P, 4])
        bias_e = sb("bias_e", [P, EXPERTS])
        bias_qk = sb("bias_qk", [P, 4])
        bias_v = sb("bias_v", [P, D])
        bias_o = sb("bias_o", [P, D])

        def const(name):
            o, n = CONSTS[name]
            return table[:, o:o + n]

        ident = const("ident")
        layer0 = whole.enter_context(ExitStack())
        w0_hi, w0_lo = (sb(f"w0_{n}", [P, WCOLS[0]], F16, layer0) for n in ("hi", "lo"))
        w_hi, w_lo = (w0_hi, w1_hi), (w0_lo, w1_lo)

        def weight(part, name, start, n):
            layer, at, _ = WEIGHTS[name]
            return part[layer][:, at + start:at + start + n]

        loaded = [sem(f"weights_loaded{i}") for i in range(STAGES)]
        consts_in = sem("consts_in")
        tanh_done = sem("tanh_done")
        setup_done = sem("setup_done")
        rounded = sem("weights_rounded")
        split = sem("weights_split")

        with ExitStack() as first:
            stage = sb("stage", [P, STAGES, STAGE[0]], to=first)
            block = first.enter_context(nc.Block())
            n = STAGE[0]

            @block.sync
            def _(sp):
                for t, src in ((table[:, :], consts), (bias_qk[:, :], bqk),
                               (bias_e[:, :], ebias.partition_broadcast(P)),
                               (bias_v[:, :], bv.partition_broadcast(P)),
                               (bias_o[:, :], bo.partition_broadcast(P)),
                               (gate_in[:, :], gates.partition_broadcast(P))):
                    sp.dma_start(t, src).then_inc(consts_in, 16)
                for s in range(STAGES):
                    sp.dma_start(stage[:, s, :], weights0[:, s * n:(s + 1) * n]).then_inc(loaded[s], 16)
                with sp.Fori(1, ROUNDS) as i:
                    for s in range(STAGES):
                        sp.wait_ge(split, i * STAGES + s - STAGES + 1)
                        sp.dma_start(stage[:, s, :], weights0[:, bass.ds(i * (STAGES * n) + s * n, n)]) \
                          .then_inc(loaded[s], 16)

            @block.scalar
            def _(act):
                act.wait_ge(consts_in, 6 * 16)
                nc.scalar.activation(tanh_g[:, :], gate_in[:, :], ACT.Tanh).then_inc(tanh_done, 1)
                with act.Fori(0, ROUNDS) as i:
                    for s in range(STAGES):
                        act.wait_ge(loaded[s], i * 16 + 16)
                        nc.scalar.activation(w0_hi[:, bass.ds(i * (STAGES * n) + s * n, n)], stage[:, s, :],
                                             ACT.Copy, scale=SW).then_inc(rounded, 1)

            @block.vector
            def _(dve):
                nc.vector.memset(minus_half[:, :], -0.5).then_inc(setup_done, 1)
                dve.wait_ge(consts_in, 6 * 16)
                nc.vector.tensor_copy(pick16[:, :], const("pick")).then_inc(setup_done, 1)
                dve.wait_ge(tanh_done, 1)
                for k, undo in enumerate((1 / SV, 1 / SW, 1.0, 1 / STEPS)):
                    nc.vector.tensor_scalar(step_of[:, k:k + 1], tanh_g[:, k:k + 1], undo, None, ALU.mult) \
                      .then_inc(setup_done, 1)
                with dve.Fori(0, ROUNDS) as i:
                    for s in range(STAGES):
                        dve.wait_ge(rounded, i * STAGES + s + 1)
                        cols = bass.ds(i * (STAGES * n) + s * n, n)
                        nc.vector.scalar_tensor_tensor(out=w0_lo[:, cols], in0=stage[:, s, :], scalar=SW,
                                                       in1=w0_hi[:, cols], op0=ALU.mult, op1=ALU.subtract) \
                          .then_inc(split, 1)

        def parts3(a_hi, a_lo, b_hi, b_lo):
            return ((a_hi, b_hi), (a_hi, b_lo), (a_lo, b_hi))

        def product(pe, dst, pairs):
            todo = [ab for a_hi, a_lo, b_hi, b_lo in pairs for ab in parts3(a_hi, a_lo, b_hi, b_lo)]
            for n, (a, b) in enumerate(todo):
                mm = pe.matmul(dst, a, b, start=n == 0, stop=n == len(todo) - 1)
            return mm

        def run(main, *sides):
            never = 1000
            slots = [next(side, never) for side in sides]

            def until(now):
                for n, side in enumerate(sides):
                    while slots[n] <= now:
                        slots[n] = next(side, never)

            for now, _ in enumerate(main):
                until(now)
            until(never - 1)

        def transposes(pe, bank, src, dt):
            for tt in range(TT):
                mm = pe.transpose(bank[:, tt * P:(tt + 1) * P], src[:, tt, dt * P:(dt + 1) * P], ident)
            return mm

        with ExitStack() as first:
            x_tok = [sb(f"x_tok{p}", [P, TT, D], to=first) for p in range(2)]
            ctx_tok = sb("ctx_tok", [P, TT, D], to=first)
            xn = sb("xn", [P, TT, D], to=first)
            stats = sb("stats", [P, TT, 6], to=first)
            moments = sb("moments", [P, TT, 2], to=first)
            var_eps = sb("var_eps", [P, TT], to=first)
            rstd = sb("rstd", [P, TT], to=first)
            xt_hi, xt_lo = (sb(f"xt_{n}", [P, DT, T], F16, first) for n in ("hi", "lo"))
            ct_hi, ct_lo = (sb(f"ct_{n}", [P, DT, T], F16, first) for n in ("hi", "lo"))
            rot = {s: sb(f"rot_{s}", [P, 4, T], to=first) for s in "qk"}
            rot_hi = {s: sb(f"rot_hi_{s}", [P, 2, T], F16, first) for s in "qk"}
            rot_lo = {s: sb(f"rot_lo_{s}", [P, 2, T], F16, first) for s in "qk"}
            v_hi, v_lo = (sb(f"v_{n}", [P, TT, D], F16, first) for n in ("hi", "lo"))
            sc_f = rot["q"][:, 2:4, :].rearrange("p b (k q) -> p b k q", k=2)
            sc_hi, sc_lo = (sb(f"sc_{n}", [P, PAIR, 2, SEQ], F16, first) for n in ("hi", "lo"))
            xf_hi, xf_lo = ([sb(f"xf_{n}{p}", [P, DT, T], F16, first) for p in range(2)] for n in ("hi", "lo"))
            logit_t = sb("logit_t", [EXPERTS, T], to=first)
            expo = sb("expo", [P, TT, EXPERTS], to=first)
            score = sb("score", [P, TT, EXPERTS], to=first)
            biased = sb("biased", [P, TT, EXPERTS], to=first)
            pair_hi = sb("pair_hi", [P, TT * EXPERT_GROUPS, 2], to=first)
            pair_lo = sb("pair_lo", [P, TT * EXPERT_GROUPS, 2], to=first)
            best = sb("best", [P, 3, TT * EXPERT_GROUPS], to=first)
            g_pad = sb("g_pad", [P, TT, 12], to=first)
            g_out = sb("g_out", [P, TT, 12], to=first)
            top8 = sb("top8", [P, TT, 8], to=first)
            g_mask = sb("g_mask", [P, TT, EXPERT_GROUPS], to=first)
            e_pad = sb("e_pad", [P, TT, EXPERTS + 2], to=first)
            e_out = sb("e_out", [P, TT, EXPERTS + 2], to=first)
            chosen = sb("chosen", [P, TT, EXPERTS], to=first)
            total = sb("total", [P, TT], to=first)
            combine = sb("combine", [P, TT, EXPERTS], to=first)
            comb_t = [sb(f"comb_t{p}", [96, T], F16, first) for p in range(2)]
            relu = sb("relu", [P, 2, T], to=first)
            gated = sb("gated", [P, 2, T], to=first)
            hid = sb("hid", [P, 3, T], to=first)
            hid_hi, hid_lo = (sb(f"hid_{n}", [P, 3, T], F16, first) for n in ("hi", "lo"))

            acc, hbank, cbank = psum[0:2], psum[2:4], psum[4]
            STEP0 = ["ctx0", "ctx1", "k0", "k1", "v0", "v1", "x0", "x1", "q0", "q1", "s0", "s1", "o0", "o1",
                     "f0", "f1", "logits", "logits_t", "comb_t"]
            FILL = {"ctx0": 0, "ctx1": 0, "k0": 2, "k1": 3, "v0": 4, "v1": 5, "x0": 7, "x1": 7, "q0": 9, "q1": 10,
                    "s0": 14, "s1": 15, "o0": 18, "o1": 19, "f0": 23, "f1": 23, "logits": 25, "logits_t": 27,
                    "comb_t": 35}
            ring = Banks(psum[5:8], sem("a_bank_full"), [sem(f"a_bank_read{b}") for b in range(3)], STEP0)
            x_in = [sem(f"a_x_in{p}") for p in range(2)]
            x_out = [sem(f"a_x_out{p}") for p in range(2)]
            ctx_in = sem("a_ctx_in")
            norm = Signal(sem("a_norm"), [f"{n}{k}" for k in range(2) for n in ("var", "xn")])
            rsqrt = Signal(sem("a_rsqrt"), ["0", "1"])
            hi_done = Signal(sem("a_hi_done"), ["ctx0", "ctx1", "v0", "k", "v1", "x0", "x1", "q", "s0", "s1",
                                                "f0", "f1", "comb"])
            lo_done = Signal(sem("a_lo_done"), ["k", "q", "s0", "s1"])
            turned = Signal(sem("a_turned"), ["k", "q"])
            combined = Signal(sem("a_combined"), [0])
            preset = sem("a_preset")
            waited = sem("a_waited")
            stage1 = [rot[s][:, :, :].rearrange("p m t -> p (m t)")[:, 0:STAGE[1]] for s in "qk"]
            loaded1 = [sem(f"a_weights1_loaded{n}") for n in range(2)]
            rounded1, split1 = sem("a_weights1_rounded"), sem("a_weights1_split")
            up_done = Signal(sem("a_up_done"), range(CHUNKS))
            relu_done = Signal(sem("a_relu_done"), range(CHUNKS))
            cb_done = Signal(sem("a_cb_done"), range(EXPERTS))
            gated_done = Signal(sem("a_gated_done"), range(EXPERTS))
            hid_done = Signal(sem("a_hid_done"), range(CHUNKS))
            hid_hi_done = Signal(sem("a_hid_hi_done"), range(CHUNKS))
            hid_lo_done = Signal(sem("a_hid_lo_done"), range(CHUNKS))
            down_done = Signal(sem("a_down_done"), range(CHUNKS))
            x_done = Signal(sem("a_x_done"), [0, 1])

            def previous(sig, g, k):
                return HEAD + g * len(sig.events) + k + 1

            block = first.enter_context(nc.Block())

            def attend_sp(sp, i, j):
                p = j
                wait(sp, x_out[p], 16 * i)
                sp.dma_start(x_tok[p][:, :, :], x[2 * i + j]).then_inc(x_in[p], 16)
                g = 2 * i + j
                if not isinstance(g, int) or g > 0:
                    ring.wait_full(sp, g - 1, "ctx1")
                sp.dma_start(ctx_tok[:, :, :], ctx[2 * i + j]).then_inc(ctx_in, 16)

            def attend_pe(pe, i, j):
                p, g = j, 2 * i + j

                def fill(step):
                    ring.wait_free(pe, g, step)
                    return ring.bank(step)

                def project(s, a_hi, a_lo, src):
                    for m in range(2):
                        yield FILL[f"{s}{m}"]
                        b = fill(f"{s}{m}")
                        for dt in range(DT):
                            ring.wait_read(pe, g, f"{src}{dt}")
                        product(pe, b[:, :], [(weight(w_hi, f"w{s}0", dt * D + m * P, P),
                                               weight(w_lo, f"w{s}0", dt * D + m * P, P),
                                               a_hi[:, dt, :], a_lo[:, dt, :]) for dt in range(DT)]) \
                            .then_inc(ring.full, 1)

                yield FILL["ctx0"]
                pe.wait_ge(ctx_in, 16 * (g + 1))
                for dt in range(DT):
                    transposes(pe, fill(f"ctx{dt}"), ctx_tok, dt).then_inc(ring.full, 1)
                yield from project("k", ct_hi, ct_lo, "ctx")
                for n in range(2):
                    yield FILL[f"v{n}"]
                    b = fill(f"v{n}")
                    for half in range(2):
                        tt = 2 * n + half
                        mm = product(pe, b[:, half * D:(half + 1) * D],
                                     [(ct_hi[:, dt, tt * P:(tt + 1) * P], ct_lo[:, dt, tt * P:(tt + 1) * P],
                                       weight(w_hi, "wv0", dt * D, D), weight(w_lo, "wv0", dt * D, D))
                                      for dt in range(DT)])
                    mm.then_inc(ring.full, 1)
                yield FILL["x0"]
                pe.wait_ge(norm.sem, norm.at(g, "xn0"))
                for dt in range(DT):
                    transposes(pe, fill(f"x{dt}"), xn, dt).then_inc(ring.full, 1)
                yield from project("q", xt_hi, xt_lo, "x")
                for b in range(PAIR):
                    yield FILL[f"s{b}"]
                    bank = fill(f"s{b}")
                    pe.wait_ge(lo_done.sem, lo_done.at(g, "q"))
                    for kt in range(2):
                        k0 = b * SEQ + kt * P
                        mm = product(pe, bank[:, kt * SEQ:(kt + 1) * SEQ],
                                     [(rot_hi["k"][:, m, k0:k0 + P], rot_lo["k"][:, m, k0:k0 + P],
                                       rot_hi["q"][:, m, b * SEQ:(b + 1) * SEQ],
                                       rot_lo["q"][:, m, b * SEQ:(b + 1) * SEQ]) for m in range(2)])
                    mm.then_inc(ring.full, 1)
                for b in range(PAIR):
                    yield FILL[f"o{b}"]
                    bank = fill(f"o{b}")
                    ring.wait_read(pe, g, f"v{b}")
                    pe.wait_ge(lo_done.sem, lo_done.at(g, f"s{b}"))
                    for qt in range(2):
                        mm = product(pe, bank[:, qt * D:(qt + 1) * D],
                                     [(sc_hi[:, b, kt, qt * P:(qt + 1) * P], sc_lo[:, b, kt, qt * P:(qt + 1) * P],
                                       v_hi[:, 2 * b + kt, :], v_lo[:, 2 * b + kt, :]) for kt in range(qt + 1)])
                    mm.then_inc(ring.full, 1)
                yield FILL["f0"]
                pe.wait_ge(norm.sem, norm.at(g, "xn1"))
                for dt in range(DT):
                    transposes(pe, fill(f"f{dt}"), xn, dt).then_inc(ring.full, 1)
                yield FILL["logits"]
                bank = fill("logits")
                for dt in range(DT):
                    ring.wait_read(pe, g, f"f{dt}")
                product(pe, bank[0:EXPERTS, :], [(weight(w_hi, "gate", dt * EXPERTS, EXPERTS),
                                                  weight(w_lo, "gate", dt * EXPERTS, EXPERTS),
                                                  xf_hi[p][:, dt, :], xf_lo[p][:, dt, :]) for dt in range(DT)]) \
                    .then_inc(ring.full, 1)
                yield FILL["logits_t"]
                bank = fill("logits_t")
                ring.wait_read(pe, g, "logits")
                pe.sem_inc(waited, 1)
                for tt in range(TT):
                    mm = pe.transpose(bank[:, tt * EXPERTS:(tt + 1) * EXPERTS], logit_t[:, tt * P:(tt + 1) * P],
                                      ident[0:EXPERTS, 0:EXPERTS])
                mm.then_inc(ring.full, 1)
                yield FILL["comb_t"]
                bank = fill("comb_t")
                pe.wait_ge(combined.sem, combined.at(g, 0))
                for tt in range(TT):
                    mm = pe.transpose(bank[0:EXPERTS, tt * P:(tt + 1) * P], combine[:, tt, :], ident)
                mm.then_inc(ring.full, 1)

            def attend_act(act, i, j):
                p, g = j, 2 * i + j

                def high(step, hi, scale):
                    yield FILL[step]
                    ring.wait_full(act, g, step)
                    nc.scalar.activation(hi, ring.bank(step)[:, :], ACT.Copy, scale=scale).then_inc(hi_done.sem, 1)

                def high_turned(s):
                    act.wait_ge(turned.sem, turned.at(g, s))
                    nc.scalar.activation(rot_hi[s][:, :, :], rot[s][:, 0:2, :], ACT.Copy).then_inc(hi_done.sem, 1)

                for dt in range(DT):
                    yield from high(f"ctx{dt}", ct_hi[:, dt, :], SX)
                yield from high("v0", v_hi[:, 0:2, :], SV / (SX * SW))
                yield FILL["k1"] + 2
                high_turned("k")
                yield from high("v1", v_hi[:, 2:4, :], SV / (SX * SW))
                for dt in range(DT):
                    yield from high(f"x{dt}", xt_hi[:, dt, :], SX)
                yield FILL["q1"] + 2
                high_turned("q")
                for b in range(PAIR):
                    yield FILL[f"s{b}"] + 1
                    ring.wait_read(act, g, f"s{b}")
                    nc.scalar.activation(sc_hi[:, b, :, :], sc_f[:, b, :, :], ACT.Copy).then_inc(hi_done.sem, 1)
                for dt in range(DT):
                    yield from high(f"f{dt}", xf_hi[p][:, dt, :], SX)
                yield FILL["logits_t"]
                ring.wait_full(act, g, "logits_t")
                nc.scalar.activation(expo[:, :, :], ring.bank("logits_t")[:, 0:TT * EXPERTS], ACT.Exp) \
                  .then_inc(ring.reader("logits_t"), 1)
                yield FILL["comb_t"]
                ring.wait_full(act, g, "comb_t")
                nc.scalar.activation(comb_t[p][0:EXPERTS, :], ring.bank("comb_t")[0:EXPERTS, :], ACT.Copy) \
                  .then_inc(hi_done.sem, 1)

            def moments_of(dve, sig, src):
                for tt in range(TT):
                    nc.vector.bn_stats(stats[:, tt, :], src[:, tt, :])
                dve.drain()
                for tt in range(TT):
                    nc.vector.bn_aggr(moments[:, tt, :], stats[:, tt, :])
                dve.drain()
                nc.vector.tensor_scalar(var_eps[:, :], moments[:, :, 1], EPS, None, ALU.add).then_inc(sig.sem, 1)

            def normalise(dve, sig, k, rs, g, src):
                dve.wait_ge(rs.sem, rs.at(g, f"{k}"))
                for tt in range(TT):
                    ins = nc.vector.tensor_scalar(xn[:, tt, :], src[:, tt, :], moments[:, tt, 0:1], rstd[:, tt:tt + 1],
                                                  ALU.subtract, ALU.mult)
                ins.then_inc(sig.sem, 1)

            def low_of_bank(dve, rg, sig, g, step, key, hi, lo, scale, cols=slice(None), rows=slice(None)):
                dve.wait_ge(sig.sem, sig.at(g, key))
                nc.vector.scalar_tensor_tensor(out=lo, in0=rg.bank(step)[rows, cols], scalar=scale, in1=hi,
                                               op0=ALU.mult, op1=ALU.subtract).then_inc(rg.reader(step), 1)

            def attend_dve(dve, i, j):
                p, g = j, 2 * i + j

                def low(step, hi, lo, scale):
                    yield FILL[step]
                    low_of_bank(dve, ring, hi_done, g, step, step, hi, lo, scale)

                def turn(s):
                    cos = const(f"c{s}").unsqueeze(1).to_broadcast([P, PAIR, SEQ])
                    sin = const(f"s{s}").unsqueeze(1).to_broadcast([P, PAIR, SEQ])
                    for m, (fa, fb) in enumerate(((cos, sin), (sin, cos))):
                        yield FILL[f"{s}{m}"]
                        ring.wait_full(dve, g, f"{s}{m}")
                        src = ring.bank(f"{s}{m}")[:, :].rearrange("p (b t) -> p b t", b=PAIR)
                        for n, f in enumerate((fa, fb)):
                            ins = nc.vector.tensor_tensor(
                                rot[s][:, 2 * m + n, :].rearrange("p (b t) -> p b t", b=PAIR), src, f, ALU.mult)
                        ins.then_inc(ring.reader(f"{s}{m}"), 1)

                def values(n):
                    yield from low(f"v{n}", v_hi[:, 2 * n:2 * n + 2, :].rearrange("p t d -> p (t d)"),
                                   v_lo[:, 2 * n:2 * n + 2, :].rearrange("p t d -> p (t d)"), SV / (SX * SW))

                for dt in range(DT):
                    yield from low(f"ctx{dt}", ct_hi[:, dt, :], ct_lo[:, dt, :], SX)
                yield from turn("k")
                yield from values(0)
                yield FILL["x0"] - 2
                dve.wait_ge(x_in[p], 16 * (i + 1))
                moments_of(dve, norm, x_tok[p])
                yield from values(1)
                yield FILL["x0"] - 1
                normalise(dve, norm, 0, rsqrt, g, x_tok[p])
                low_of_turned(dve, g, "k")
                for dt in range(DT):
                    yield from low(f"x{dt}", xt_hi[:, dt, :], xt_lo[:, dt, :], SX)
                yield from turn("q")
                yield FILL["q1"] + 3
                low_of_turned(dve, g, "q")
                for b in range(PAIR):
                    yield FILL[f"s{b}"]
                    ring.wait_full(dve, g, f"s{b}")
                    nc.vector.tensor_tensor(sc_f[:, b, :, :].rearrange("p k q -> p (k q)"), ring.bank(f"s{b}")[:, :],
                                            const("decay"), ALU.mult).then_inc(ring.reader(f"s{b}"), 1)
                for b in range(PAIR):
                    yield FILL[f"s{b}"] + 2
                    dve.wait_ge(hi_done.sem, hi_done.at(g, f"s{b}"))
                    nc.vector.tensor_tensor(sc_lo[:, b, :, :], sc_f[:, b, :, :], sc_hi[:, b, :, :], ALU.subtract) \
                      .then_inc(lo_done.sem, 1)
                for b in range(PAIR):
                    yield FILL[f"o{b}"]
                    ring.wait_full(dve, g, f"o{b}")
                    xs = x_tok[p][:, 2 * b:2 * b + 2, :].rearrange("p t d -> p (t d)")
                    nc.vector.scalar_tensor_tensor(out=xs, in0=ring.bank(f"o{b}")[:, :], scalar=step_of[:, 0:1], in1=xs,
                                                   op0=ALU.mult, op1=ALU.add).then_inc(ring.reader(f"o{b}"), 1)
                yield FILL["o1"] + 1
                for b in range(PAIR):
                    ring.wait_read(dve, g, f"o{b}")
                moments_of(dve, norm, x_tok[p])
                yield FILL["o1"] + 2
                normalise(dve, norm, 1, rsqrt, g, x_tok[p])
                for dt in range(DT):
                    yield from low(f"f{dt}", xf_hi[p][:, dt, :], xf_lo[p][:, dt, :], SX)
                yield FILL["logits"]
                ring.wait_full(dve, g, "logits")
                nc.vector.tensor_scalar(logit_t[:, :], ring.bank("logits")[0:EXPERTS, :], -1 / (SX * SW), 88.0,
                                        ALU.mult, ALU.min).then_inc(ring.reader("logits"), 1)
                for n, _ in enumerate(router(dve, g)):
                    yield FILL["logits_t"] + 1 + n
                yield FILL["comb_t"]
                low_of_bank(dve, ring, hi_done, g, "comb_t", "comb", comb_t[p][0:EXPERTS, :],
                            comb_t[p][EXPERTS:2 * EXPERTS, :], 1.0, rows=slice(0, EXPERTS))

            def low_of_turned(dve, g, s):
                dve.wait_ge(hi_done.sem, hi_done.at(g, s))
                nc.vector.tensor_tensor(rot_lo[s][:, :, :], rot[s][:, 0:2, :], rot_hi[s][:, :, :], ALU.subtract) \
                  .then_inc(lo_done.sem, 1)

            def router(dve, g):
                V = nc.vector

                def done(ins):
                    dve.drain()

                yield
                ring.wait_read(dve, g, "logits_t")
                done(V.tensor_scalar(expo[:, :, :], expo[:, :, :], 1.0, None, ALU.add))
                done(V.reciprocal(score[:, :, :], expo[:, :, :]))
                done(V.tensor_tensor(biased[:, :, :], score[:, :, :],
                                     bias_e[:, :].unsqueeze(1).to_broadcast([P, TT, EXPERTS]), ALU.add))
                yield
                four = biased[:, :, :].rearrange("p t (g f) -> p (t g) f", f=4)
                V.tensor_tensor(pair_hi[:, :, :], four[:, :, 0:2], four[:, :, 2:4], ALU.max)
                done(V.tensor_tensor(pair_lo[:, :, :], four[:, :, 0:2], four[:, :, 2:4], ALU.min))
                V.tensor_tensor(best[:, 0, :], pair_hi[:, :, 0], pair_hi[:, :, 1], ALU.max)
                V.tensor_tensor(best[:, 1, :], pair_hi[:, :, 0], pair_hi[:, :, 1], ALU.min)
                done(V.tensor_tensor(best[:, 2, :], pair_lo[:, :, 0], pair_lo[:, :, 1], ALU.max))
                done(V.tensor_tensor(best[:, 1, :], best[:, 1, :], best[:, 2, :], ALU.max))
                done(V.tensor_tensor(g_pad[:, :, 0:EXPERT_GROUPS], best[:, 0, :].rearrange("p (t g) -> p t g", t=TT),
                                     best[:, 1, :].rearrange("p (t g) -> p t g", t=TT), ALU.add))
                yield
                for tt in range(TT):
                    ins = V.max(top8[:, tt, :], g_pad[:, tt, :])
                done(ins)
                for tt in range(TT):
                    ins = V.match_replace(g_out[:, tt, :], top8[:, tt, :], g_pad[:, tt, :], -BIG)
                done(ins)
                yield
                done(V.tensor_scalar(g_mask[:, :, :], g_out[:, :, 0:EXPERT_GROUPS], -BIG, None, ALU.is_equal))
                for tt in range(TT):
                    ins = V.tensor_tensor(e_pad[:, tt, 0:EXPERTS].rearrange("p (g f) -> p g f", f=4),
                                          biased[:, tt, :].rearrange("p (g f) -> p g f", f=4),
                                          g_mask[:, tt, :].unsqueeze(2).to_broadcast([P, EXPERT_GROUPS, 4]), ALU.mult)
                done(ins)
                yield
                for tt in range(TT):
                    ins = V.max(top8[:, tt, :], e_pad[:, tt, :])
                done(ins)
                for tt in range(TT):
                    ins = V.match_replace(e_out[:, tt, :], top8[:, tt, :], e_pad[:, tt, :], -BIG)
                done(ins)
                yield
                done(V.scalar_tensor_tensor(out=chosen[:, :, :], in0=e_out[:, :, 0:EXPERTS], scalar=-BIG,
                                            in1=score[:, :, :], op0=ALU.is_equal, op1=ALU.mult))
                done(V.tensor_reduce(total[:, :], chosen[:, :, :], AX_X, ALU.add))
                done(V.tensor_scalar(total[:, :], total[:, :], 1e-20, None, ALU.add))
                done(V.reciprocal(total[:, :], total[:, :]))
                V.scalar_tensor_tensor(out=combine[:, :, :], in0=chosen[:, :, :], scalar=ROUTED_SCALE,
                                            in1=total[:, :].unsqueeze(2).to_broadcast([P, TT, EXPERTS]),
                                            op0=ALU.mult, op1=ALU.mult).then_inc(combined.sem, 1)

            def attend_pool(pool, i, j):
                g = 2 * i + j

                def power(k):
                    pool.wait_ge(norm.sem, norm.at(g, f"var{k}"))
                    nc.gpsimd.tensor_tensor(rstd[:, :], var_eps[:, :], minus_half[:, :], ALU.pow) \
                      .then_inc(rsqrt.sem, 1)

                def turn(s):
                    for m in range(2):
                        ring.wait_read(pool, g, f"{s}{m}")
                    nc.gpsimd.tensor_tensor(rot[s][:, 0, :], rot[s][:, 0, :], rot[s][:, 2, :], ALU.subtract)
                    nc.gpsimd.tensor_tensor(rot[s][:, 1, :], rot[s][:, 1, :], rot[s][:, 3, :], ALU.add) \
                      .then_inc(turned.sem, 1)

                yield FILL["k1"] + 1
                turn("k")
                yield FILL["x0"] - 2
                power(0)
                yield FILL["q1"] + 1
                turn("q")
                yield FILL["o1"] + 1
                power(1)

            def experts_pe(pe, i, j):
                p, g = j, 2 * i + j

                def up(e):
                    wait(pe, relu_done.sem, previous(relu_done, g, e - 2))
                    product(pe, hbank[e % 2][:, :],
                            [(weight(w_hi, "up", (e * DT + dt) * P, P), weight(w_lo, "up", (e * DT + dt) * P, P),
                              xf_hi[p][:, dt, :], xf_lo[p][:, dt, :]) for dt in range(DT)]).then_inc(up_done.sem, 1)

                def spread(e):
                    wait(pe, gated_done.sem, previous(gated_done, g, e - 1))
                    pe.matmul(cbank[:, :], pick16[0:96, e:e + 1].to_broadcast([96, P]), comb_t[p][:, :],
                              start=True, stop=True).then_inc(cb_done.sem, 1)

                def down(e):
                    pe.wait_ge(hid_lo_done.sem, hid_lo_done.at(g, e))
                    if e == 0:
                        wait(pe, x_done.sem, previous(x_done, g, -1))
                    for tt in range(TT):
                        hi, lo = (h[:, e % 3, tt * P:(tt + 1) * P] for h in (hid_hi, hid_lo))
                        for n, (a, b) in enumerate(parts3(hi, lo, weight(w_hi, "down", e * D, D),
                                                          weight(w_lo, "down", e * D, D))):
                            mm = pe.matmul(acc[tt // 2][:, (tt % 2) * D:(tt % 2 + 1) * D], a, b,
                                           start=e == 0 and n == 0 and tt % 2 == 0,
                                           stop=e == CHUNKS - 1 and n == 2, skip_group_check=True)
                    mm.then_inc(down_done.sem, 1)

                for dt in range(DT):
                    ring.wait_read(pe, g, f"f{dt}")
                for e in range(CHUNKS + 2):
                    if e < CHUNKS:
                        up(e)
                    if e == 0:
                        ring.wait_read(pe, g, "comb_t")
                    if e < EXPERTS:
                        spread(e)
                    if e >= 2:
                        down(e - 2)
                    yield

            def experts_act(act, i, j):
                g = 2 * i + j
                for e in range(CHUNKS + 1):
                    if e < CHUNKS:
                        act.wait_ge(up_done.sem, up_done.at(g, e))
                        wait(act, hid_done.sem, previous(hid_done, g, e - 2))
                        nc.scalar.activation(relu[:, e % 2, :], hbank[e % 2][:, :], ACT.Relu, scale=1 / (SX * SW)) \
                          .then_inc(relu_done.sem, 1)
                    if e >= 1:
                        act.wait_ge(hid_done.sem, hid_done.at(g, e - 1))
                        wait(act, down_done.sem, previous(down_done, g, e - 4))
                        nc.scalar.activation(hid_hi[:, (e - 1) % 3, :], hid[:, (e - 1) % 3, :], ACT.Copy) \
                          .then_inc(hid_hi_done.sem, 1)
                    yield

            def experts_dve(dve, i, j):
                p, g = j, 2 * i + j
                for e in range(CHUNKS + 1):
                    if e < EXPERTS:
                        dve.wait_ge(relu_done.sem, relu_done.at(g, e))
                        dve.wait_ge(cb_done.sem, cb_done.at(g, e))
                        wait(dve, hid_done.sem, previous(hid_done, g, e - 2))
                        nc.vector.tensor_tensor(gated[:, e % 2, :], relu[:, e % 2, :], cbank[:, :], ALU.mult) \
                          .then_inc(gated_done.sem, 1)
                    if e >= 1:
                        dve.wait_ge(hid_hi_done.sem, hid_hi_done.at(g, e - 1))
                        nc.vector.tensor_tensor(hid_lo[:, (e - 1) % 3, :], hid[:, (e - 1) % 3, :],
                                                hid_hi[:, (e - 1) % 3, :], ALU.subtract).then_inc(hid_lo_done.sem, 1)
                    yield
                dve.wait_ge(down_done.sem, down_done.at(g, CHUNKS - 1))
                for n in range(2):
                    xs = x_tok[p][:, 2 * n:2 * n + 2, :].rearrange("p t d -> p (t d)")
                    nc.vector.scalar_tensor_tensor(out=xs, in0=acc[n][:, :], scalar=step_of[:, 1:2], in1=xs,
                                                   op0=ALU.mult, op1=ALU.add).then_inc(x_done.sem, 1)
                yield

            def experts_pool(pool, i, j):
                g = 2 * i + j
                for e in range(CHUNKS):
                    if e < EXPERTS:
                        pool.wait_ge(gated_done.sem, gated_done.at(g, e))
                    else:
                        pool.wait_ge(relu_done.sem, relu_done.at(g, e))
                    wait(pool, hid_lo_done.sem, previous(hid_lo_done, g, e - 3))
                    by = gated if e < EXPERTS else relu
                    nc.gpsimd.tensor_tensor(hid[:, e % 3, :], relu[:, e % 2, :], by[:, e % 2, :], ALU.mult) \
                      .then_inc(hid_done.sem, 1)
                    yield

            def experts_sp(sp, i, j):
                g = 2 * i + j
                sp.wait_ge(x_done.sem, x_done.at(g, 1))
                sp.dma_start(x_mid[g], x_tok[j][:, :, :]).then_inc(x_out[j], 16)

            def weights1_sp(sp):
                n = STAGE[1]
                sp.wait_ge(lo_done.sem, lo_done.at(GROUPS - 1, "q"))
                for i in range(PIECES1):
                    wait(sp, split1, i - 1)
                    sp.dma_start(stage1[i % 2], weights1[:, i * n:(i + 1) * n]).then_inc(loaded1[i % 2], 16)

            def weights1_act(act):
                n = STAGE[1]
                for i in range(PIECES1):
                    yield 3 + 5 * i
                    act.wait_ge(loaded1[i % 2], i // 2 * 16 + 16)
                    nc.scalar.activation(w1_hi[:, i * n:(i + 1) * n], stage1[i % 2], ACT.Copy, scale=SW) \
                      .then_inc(rounded1, 1)

            def weights1_dve(dve):
                n = STAGE[1]
                for i in range(PIECES1):
                    yield 4 + 5 * i
                    dve.wait_ge(rounded1, i + 1)
                    nc.vector.scalar_tensor_tensor(out=w1_lo[:, i * n:(i + 1) * n], in0=stage1[i % 2], scalar=SW,
                                                   in1=w1_hi[:, i * n:(i + 1) * n], op0=ALU.mult, op1=ALU.subtract) \
                      .then_inc(split1, 1)

            def both(eng, attend, experts, beside_last=lambda eng: iter(())):
                for _ in attend(eng, 0, 0):
                    pass
                with eng.Fori(0, GROUPS // 2 - 1) as i:
                    for j in range(2):
                        run(experts(eng, i, j), attend(eng, i + j, 1 - j))
                last = GROUPS // 2 - 1
                run(experts(eng, last, 0), attend(eng, last, 1))
                run(experts(eng, last, 1), beside_last(eng))

            @block.sync
            def _(sp):
                attend_sp(sp, 0, 0)
                attend_sp(sp, 0, 1)
                with sp.Fori(0, GROUPS // 2 - 1) as i:
                    for j in range(2):
                        experts_sp(sp, i, j)
                        attend_sp(sp, i + 1, j)
                experts_sp(sp, GROUPS // 2 - 1, 0)
                weights1_sp(sp)
                experts_sp(sp, GROUPS // 2 - 1, 1)
                for j in range(2):
                    sp.wait_ge(x_out[j], 16 * (GROUPS // 2))

            @block.tensor
            def _(pe):
                pe.wait_ge(preset, 1)
                both(pe, attend_pe, experts_pe)

            @block.scalar
            def _(act):
                both(act, attend_act, experts_act, weights1_act)

            @block.vector
            def _(dve):
                for p in range(2):
                    nc.vector.memset(comb_t[p][64:96, :], 0.0)
                nc.vector.memset(g_pad[:, :, EXPERT_GROUPS:], BIG)
                nc.vector.memset(e_pad[:, :, EXPERTS:], BIG).then_inc(preset, 1)
                dve.wait_ge(preset, 1)
                both(dve, attend_dve, experts_dve, weights1_dve)

            @block.gpsimd
            def _(pool):
                for s in (norm, rsqrt, hi_done, lo_done, turned, combined, up_done, relu_done, cb_done, gated_done,
                          hid_done, hid_hi_done, hid_lo_done, down_done, x_done):
                    pool.sem_inc(s.sem, HEAD)
                for s in ring.read:
                    pool.sem_inc(s, HEAD)
                both(pool, attend_pool, experts_pool)

        layer0.close()

        with ExitStack() as second:
            x_tok = sb("x1_tok", [P, TT, D], to=second)
            x_res = [sb(f"x1_res{p}", [P, TT, D], to=second) for p in range(2)]
            ctx_tok = sb("ctx1_tok", [P, TT, D], to=second)
            xn = sb("xn1", [P, TT, D], to=second)
            stats = sb("stats1", [P, TT, 6], to=second)
            moments = sb("moments1", [P, TT, 2], to=second)
            var_eps = sb("var_eps1", [P, TT], to=second)
            rstd = sb("rstd1", [P, TT], to=second)
            xt_hi, xt_lo = (sb(f"xt1_{n}", [P, DT, T], F16, second) for n in ("hi", "lo"))
            ct_hi, ct_lo = (sb(f"ct1_{n}", [P, DT, T], F16, second) for n in ("hi", "lo"))
            qk = sb("qk", [P, 2, T], to=second)
            qk_hi, qk_lo = ([sb(f"qk_{n}{p}", [P, 4, T], F16, second) for p in range(2)] for n in ("hi", "lo"))
            v_one = [sb(f"v_one{p}", [P, TT, HEADS, 2 * HD], to=second) for p in range(2)]
            q_stack, k_stack = ([sb(f"{n}_stack{b}", [P, HEADS, SEQ], F16, second) for b in range(PAIR)] for n in "qk")
            row_max = sb("row_max", [P, 2, HEADS], to=second)
            max_hi, max_lo = (sb(f"max_{n}", [HEADS, SEQ], F16, second) for n in ("hi", "lo"))
            NPR = 4
            prob = sb("prob", [P, NPR, 2, SEQ], to=second)
            mixed = sb("mixed", [P, 2, 2 * SEQ], to=second)
            den = sb("den_rows", [P, 4 * 4 * SEQ // P], to=second)
            den_inv = sb("den_inv", [P, 4 * 4 * SEQ // P], to=second)
            inverse = sb("inverse", [P, 2, 2 * SEQ], to=second)
            att = sb("att", [P, 2, 2 * SEQ], to=second)
            att_hi, att_lo = (sb(f"att_{n}", [P, 4, SEQ], F16, second) for n in ("hi", "lo"))
            proj = sb("proj", [P, 2, D], to=second)
            xf_hi, xf_lo = (sb(f"xf1_{n}", [P, DT, T], F16, second) for n in ("hi", "lo"))
            relu = sb("relu1", [P, 2, T], to=second)
            hid = sb("hid1", [P, 2, T], to=second)
            hid_hi, hid_lo = (sb(f"hid1_{n}", [P, 2, T], F16, second) for n in ("hi", "lo"))
            drive, leak, spike, spikes = (sb(n, [P, TT * D], to=second) for n in ("drive", "leak", "spike", "spikes"))
            mem = [sb(f"mem{k}", [P, TT * D], to=second) for k in range(2)]

            acc, ubank = psum[0:2], psum[2]
            heads = range(HEADS)
            ROW = HEADS + 5
            SLOTS = PAIR * ROW
            MIX_LAG = 2
            firsts = Banks(psum[3:5], sem("b_first_full"), [sem(f"b_first_read{b}") for b in range(2)],
                           [s for b in range(PAIR) for s in (*(f"{b}max{h}" for h in heads), f"{b}turn")])
            seconds = Banks(psum[5:6], sem("b_second_full"), [sem("b_second_read")],
                            [f"{b}exp{h}" for b in range(PAIR) for h in heads])
            FRONT = {s: 2 + 2 * n for n, s in enumerate(("ctx0", "ctx1", "k0", "k1", "x0", "x1", "q0", "q1", "v0", "v1"))}
            front = Banks(psum[6:7], sem("b_front_full"), [sem("b_front_read")], list(FRONT))
            MIXED = tuple((b + 2) * ROW for b in range(PAIR))
            DIVIDE = (MIXED[0] + 5, MIXED[1] + 6)
            WO = (DIVIDE[1] - 1, DIVIDE[1] + 3)
            NORM, F_AT, UP_AT, UP_STEP, DOWN_LAG = WO[1] + 2, WO[1] + 5, WO[1] + 9, 4, 6
            DRIVE_AT = UP_AT + UP_STEP * (FC - 1) + DOWN_LAG + 1
            FIRE_STEP = 3

            def fire_slot(k, c):
                return DRIVE_AT + 4 + FIRE_STEP * (2 * (k - 2) + c) // 2

            FIRED_AT = fire_slot(STEPS, 1) + 2
            tail = Banks(psum[7:8], sem("b_tail_full"), [sem("b_tail_read")],
                         ["wo0", "wo1", "f0", "f1"] + [f"up{f}" for f in range(FC)])
            TAIL_TURNS = (FIRED_AT + 1) // SLOTS

            x_in, ctx_in, res_in, x_out = (sem(f"b_{n}") for n in ("x_in", "ctx_in", "res_in", "x_out"))
            norm = Signal(sem("b_norm"), ["var0", "xn0"])
            norm_f = Signal(sem("b_norm_f"), ["var0", "xn0"])
            rsqrt, rsqrt_f = Signal(sem("b_rsqrt"), ["0"]), Signal(sem("b_rsqrt_f"), ["0"])
            front_hi = Signal(sem("b_front_hi"), ["ctx0", "ctx1", "k0", "k1", "x0", "x1", "q0", "q1"])
            front_lo = Signal(sem("b_front_lo"), ["k0", "k1", "q0", "q1"])
            values = Signal(sem("b_values"), range(TT))
            stacked = [sem(f"b_stacked{b}") for b in range(PAIR)]
            STACKED = 6 * 16
            max_high = Signal(sem("b_max_high"), ["0max", "1max"])
            max_stacked = sem("b_max_stacked")
            mixing = Signal(sem("b_mixing"), [f"{b}head{h}" for b in range(PAIR) for h in heads])
            mix_read = Signal(sem("b_mix_read"), [f"{b}{n}" for b in range(PAIR) for n in range(2)])
            den_in, den_saved, inverse_in = sem("b_den_in"), sem("b_den_saved"), sem("b_inverse_in")
            inverted = Signal(sem("b_inverted"), range(PAIR))
            att_done = Signal(sem("b_att_done"), range(PAIR))
            att_high = Signal(sem("b_att_high"), range(PAIR))
            att_low = Signal(sem("b_att_low"), range(PAIR))
            x_mixed = Signal(sem("b_x_mixed"), range(PAIR))
            tail_hi = Signal(sem("b_tail_hi"), ["f0", "f1"])
            hid_done = Signal(sem("b_hid_done"), range(FC))
            hid_hi_done = Signal(sem("b_hid_hi_done"), range(FC))
            hid_lo_done = Signal(sem("b_hid_lo_done"), range(FC))
            down_done = Signal(sem("b_down_done"), range(FC))
            driven = Signal(sem("b_driven"), range(2))
            potential = Signal(sem("b_potential"), [(k, c) for k in range(2, STEPS + 1) for c in range(2)])
            over = Signal(sem("b_over"), [(k, c) for k in range(2, STEPS + 1) for c in range(2)])
            counted = Signal(sem("b_counted"), [(k, c) for k in range(1, STEPS + 1) for c in range(2)])
            fired = Signal(sem("b_fired"), [0])
            zeroed, preset = sem("b_zeroed"), sem("b_preset")
            passed, pool_passed = sem("b_passed"), sem("b_pool_passed")
            heads_start = (norm, norm_f, rsqrt, rsqrt_f, front_hi, front_lo, values, max_high, mixing, mix_read,
                           inverted, att_done, att_high, att_low, x_mixed, tail_hi, hid_done, hid_hi_done,
                           hid_lo_done, down_done, driven, potential, over, counted, fired)

            block = second.enter_context(nc.Block())

            def exists(g, first=0):
                return not isinstance(g, int) or first <= g < GROUPS

            def groups(eng, front_of, attention_of, tail_of, before_attention=lambda: None):
                def beside(g, p):
                    sides = [tail_of(eng, g - turn, (p + turn) % 2, turn)
                             for turn in range(TAIL_TURNS, 0, -1) if exists(g - turn)]
                    if exists(g + 1):
                        sides.append(front_of(eng, g + 1, 1 - p))
                    run(attention_of(eng, g, p), *sides)

                run(iter(()), front_of(eng, 0, 0))
                before_attention()
                for g in range(TAIL_TURNS):
                    beside(g, g % 2)
                with eng.Fori(0, (GROUPS - 1 - TAIL_TURNS) // 2) as i:
                    for k in range(TAIL_TURNS, TAIL_TURNS + 2):
                        beside(i * 2 + k, k % 2)
                for g in range(GROUPS - 1, GROUPS + TAIL_TURNS):
                    beside(g, g % 2)

            def in_turn(turn, steps):
                for slot, work, *args in sorted(steps, key=lambda s: s[0]):
                    if slot // SLOTS == turn:
                        yield slot % SLOTS
                        work(*args)

            def load(sp, g):
                sp.dma_start(ctx_tok[:, :, :], ctx[g]).then_inc(ctx_in, 16)
                sp.dma_start(x_tok[:, :, :], x_mid[g]).then_inc(x_in, 16)

            def stack(sp, g, p, b):
                for stack, first_tile, roles in ((k_stack, 0, (qk_hi, qk_hi, qk_lo)), (q_stack, 2, (qk_hi, qk_lo, qk_hi))):
                    for r, part in enumerate(roles):
                        sp.dma_start(stack[b][r * HD:(r + 1) * HD, :, :],
                                     part[p][:, first_tile:first_tile + 2, b * SEQ:(b + 1) * SEQ]).then_inc(stacked[b], 16)

            def stack_max(sp, g, b):
                firsts.wait_read(sp, g, f"{b}turn")
                sp.dma_start(q_stack[b][96:97, :, :], max_hi[:, :]).then_inc(max_stacked, 16)
                sp.dma_start(q_stack[b][97:98, :, :], max_lo[:, :]).then_inc(max_stacked, 16)

            def invert(sp, g, b):
                n = g * PAIR + b + 1
                sp.wait_ge(mix_read.sem, mix_read.at(g, f"{b}1"))
                sp.dma_start(den[:, :], mixed[HD:HD + 97:32, :, :]).then_inc(den_in, 16)
                sp.wait_ge(inverted.sem, inverted.at(g, b))
                sp.dma_start(den_mid[b].rearrange("c (r k) -> (c r) k", k=den.shape[1]), den_inv[:, :]).then_inc(den_saved, 16)
                sp.wait_ge(den_saved, 16 * n)
                for c in range(4):
                    sp.dma_start(inverse[32 * c:32 * c + 32, :, :].rearrange("p n q -> p (n q)"),
                                 den_mid[b, c].partition_broadcast(32)).then_inc(inverse_in, 16)

            @block.sync
            def _(sp):
                load(sp, 0)
                sp.wait_ge(zeroed, 4)

                def stacks(g, p, b):
                    sp.wait_ge(front_lo.sem, front_lo.at(g, "q1"))
                    if exists(g - 1):
                        sp.sem_inc(passed, 1)
                        seconds.wait_full(sp, g - 1, f"{b}exp{HEADS - 1}")
                    stack(sp, g, p, b)

                def beside(g, p):
                    if exists(g - 1):
                        stack_max(sp, g - 1, 0)
                    if exists(g + 1):
                        sp.wait_ge(norm.sem, norm.at(g, "xn0"))
                        sp.sem_inc(passed, 1)
                        front.wait_full(sp, g, "ctx1")
                        load(sp, g + 1)
                    if exists(g - 2):
                        invert(sp, g - 2, 1)
                    if exists(g):
                        stacks(g, p, 0)
                    if exists(g - 1):
                        stack_max(sp, g - 1, 1)
                        invert(sp, g - 1, 0)
                    if exists(g):
                        stacks(g, p, 1)
                for g in range(TAIL_TURNS):
                    beside(g, g % 2)
                with sp.Fori(0, (GROUPS - 1 - TAIL_TURNS) // 2) as i:
                    for k in range(TAIL_TURNS, TAIL_TURNS + 2):
                        beside(i * 2 + k, k % 2)
                for g in range(GROUPS - 1, GROUPS + 3):
                    beside(g, g % 2)
                sp.wait_ge(x_out, HEAD + 16 * GROUPS)

            def front_pe(pe, g, p):
                def fill(step):
                    front.wait_free(pe, g, step)
                    return front.bank(step)

                for dt in range(DT):
                    yield FRONT[f"ctx{dt}"]
                    if dt == 0:
                        pe.wait_ge(ctx_in, 16 * (g + 1))
                    transposes(pe, fill(f"ctx{dt}"), ctx_tok, dt).then_inc(front.full, 1)

                def project(s, a_hi, a_lo, src):
                    for m in range(2):
                        yield FRONT[f"{s}{m}"]
                        b = fill(f"{s}{m}")
                        front.wait_read(pe, g, f"{src}1")
                        product(pe, b[:, :], [(weight(w_hi, f"w{s}1", dt * D + m * P, P),
                                               weight(w_lo, f"w{s}1", dt * D + m * P, P),
                                               a_hi[:, dt, :], a_lo[:, dt, :]) for dt in range(DT)]) \
                            .then_inc(front.full, 1)

                yield from project("k", ct_hi, ct_lo, "ctx")
                for dt in range(DT):
                    yield FRONT[f"x{dt}"]
                    pe.wait_ge(norm.sem, norm.at(g, "xn0"))
                    transposes(pe, fill(f"x{dt}"), xn, dt).then_inc(front.full, 1)
                yield from project("q", xt_hi, xt_lo, "x")
                for n in range(2):
                    yield FRONT[f"v{n}"]
                    b = fill(f"v{n}")
                    for half in range(2):
                        tt = 2 * n + half
                        mm = product(pe, b[:, half * D:(half + 1) * D],
                                     [(ct_hi[:, dt, tt * P:(tt + 1) * P], ct_lo[:, dt, tt * P:(tt + 1) * P],
                                       weight(w_hi, "wv1", dt * D, D), weight(w_lo, "wv1", dt * D, D))
                                      for dt in range(DT)])
                    mm.then_inc(front.full, 1)

            def attention_pe(pe, g, p):
                def maxima(b, h):
                    if h == 0:
                        pe.wait_ge(stacked[b], (g + 1) * STACKED)
                    firsts.wait_free(pe, g, f"{b}max{h}")
                    bank = firsts.bank(f"{b}max{h}")
                    for qt in range(2):
                        mm = pe.matmul(bank[:, qt * SEQ:(qt + 1) * SEQ], q_stack[b][0:96, h, qt * P:(qt + 1) * P],
                                       k_stack[b][0:96, h, :], start=True, stop=True)
                    mm.then_inc(firsts.full, 1)

                def turn(b):
                    for h in (HEADS - 2, HEADS - 1):
                        firsts.wait_read(pe, g, f"{b}max{h}")
                    bank = firsts.bank(f"{b}turn")
                    for qt in range(2):
                        mm = pe.transpose(bank[0:HEADS, qt * P:(qt + 1) * P], row_max[:, qt, :], ident)
                    mm.then_inc(firsts.full, 1)

                def scores(g, b, h):
                    if h == 0:
                        pe.wait_ge(max_stacked, (g * PAIR + b + 1) * 32)
                    seconds.wait_free(pe, g, f"{b}exp{h}")
                    bank = seconds.bank(f"{b}exp{h}")
                    for kt in range(2):
                        mm = pe.matmul(bank[:, kt * SEQ:(kt + 1) * SEQ], k_stack[b][0:98, h, kt * P:(kt + 1) * P],
                                       q_stack[b][0:98, h, :], start=True, stop=True)
                    mm.then_inc(seconds.full, 1)

                def mix(g, p, b, h):
                    n, half, c = h // 8, (h // 4) % 2, h % 4
                    if h == 0:
                        pe.wait_ge(values.sem, values.at(g, 2 * b + 1))
                    if h % 8 == 0:
                        pe.wait_ge(mix_read.sem, mix_read.at(g, f"{b}{n}") - 1)
                    seconds.wait_read(pe, g, f"{b}exp{h}")
                    for kt in range(2):
                        mm = pe.matmul(ubank[32 * c:32 * c + 32, half * SEQ:(half + 1) * SEQ],
                                       v_one[p][:, 2 * b + kt, h, :], prob[:, h % NPR, kt, :],
                                       start=kt == 0, stop=kt == 1, tile_position=(0, 32 * c))
                    mm.then_inc(mixing.sem, 1)

                for s in range(SLOTS):
                    b, h = divmod(s, ROW)
                    before = (g, p, 0) if b == 1 else (g - 1, 1 - p, 1)
                    if exists(before[0]) and h in heads:
                        scores(before[0], before[2], h)
                    if exists(before[0]) and h - MIX_LAG in heads:
                        mix(*before, h - MIX_LAG)
                    if exists(g) and h in heads:
                        maxima(b, h)
                    if exists(g) and h == HEADS:
                        turn(b)
                    yield

            def project_out(pe, g, b):
                tail.wait_free(pe, g, f"wo{b}")
                pe.wait_ge(att_low.sem, att_low.at(g, b))
                for qt in range(2):
                    mm = product(pe, tail.bank(f"wo{b}")[:, qt * D:(qt + 1) * D],
                                 [(att_hi[:, n, qt * P:(qt + 1) * P], att_lo[:, n, qt * P:(qt + 1) * P],
                                   weight(w_hi, "wo", n * D, D), weight(w_lo, "wo", n * D, D)) for n in range(4)])
                mm.then_inc(tail.full, 1)

            def tail_pe(pe, g, p, turn):
                def turn_f(dt):
                    if dt == 0:
                        pe.wait_ge(norm_f.sem, norm_f.at(g, "xn0"))
                    tail.wait_free(pe, g, f"f{dt}")
                    transposes(pe, tail.bank(f"f{dt}"), xn, dt).then_inc(tail.full, 1)

                def up(f):
                    tail.wait_free(pe, g, f"up{f}")
                    product(pe, tail.bank(f"up{f}")[:, :],
                            [(weight(w_hi, "fc", (f * DT + dt) * P, P), weight(w_lo, "fc", (f * DT + dt) * P, P),
                              xf_hi[:, dt, :], xf_lo[:, dt, :]) for dt in range(DT)]).then_inc(tail.full, 1)

                def down(f):
                    if f == 0:
                        pe.wait_ge(driven.sem, driven.at(g, 1) - 2)
                    pe.wait_ge(hid_lo_done.sem, hid_lo_done.at(g, f))
                    for tt in range(TT):
                        hi, lo = (h[:, f % 2, tt * P:(tt + 1) * P] for h in (hid_hi, hid_lo))
                        for n, (a, b) in enumerate(parts3(hi, lo, weight(w_hi, "proj", f * D, D),
                                                          weight(w_lo, "proj", f * D, D))):
                            mm = pe.matmul(acc[tt // 2][:, (tt % 2) * D:(tt % 2 + 1) * D], a, b,
                                           start=f == 0 and n == 0 and tt % 2 == 0,
                                           stop=f == FC - 1 and n == 2, skip_group_check=True)
                    mm.then_inc(down_done.sem, 1)

                yield from in_turn(turn, [(WO[b], project_out, pe, g, b) for b in range(PAIR)]
                                   + [(F_AT + 2 * dt, turn_f, dt) for dt in range(DT)]
                                   + [(UP_AT + UP_STEP * f, up, f) for f in range(FC)]
                                   + [(UP_AT + UP_STEP * f + DOWN_LAG, down, f) for f in range(FC)])

            @block.tensor
            def _(pe):
                groups(pe, front_pe, attention_pe, tail_pe, lambda: pe.wait_ge(preset, 3))

            def front_act(act, g, p):
                def high(step, hi):
                    yield FRONT[step]
                    front.wait_full(act, g, step)
                    nc.scalar.activation(hi, front.bank(step)[:, :], ACT.Copy, scale=SX).then_inc(front_hi.sem, 1)

                def biased(first, s, n):
                    for m in range(2):
                        yield FRONT[f"{s}{m}"]
                        front.wait_full(act, g, f"{s}{m}")
                        nc.scalar.activation(qk[:, m, :], front.bank(f"{s}{m}")[:, :], ACT.Identity,
                                             bias=bias_qk[:, n + m:n + m + 1], scale=1 / (SX * SW)) \
                          .then_inc(front.reader(f"{s}{m}"), 1)
                        front.wait_read(act, g, f"{s}{m}")
                        if s == "k":
                            for st in stacked:
                                wait(act, st, (g - 1) * STACKED)
                        nc.scalar.activation(qk_hi[p][:, first + m, :], qk[:, m, :], ACT.Copy).then_inc(front_hi.sem, 1)

                for dt in range(DT):
                    yield from high(f"ctx{dt}", ct_hi[:, dt, :])
                yield from biased(0, "k", 2)
                for dt in range(DT):
                    yield from high(f"x{dt}", xt_hi[:, dt, :])
                yield from biased(2, "q", 0)

            def attention_act(act, g, p):
                def evacuate(g, b, n):
                    act.wait_ge(mixing.sem, mixing.at(g, f"{b}head{8 * n + 7}"))
                    act.wait_ge(att_done.sem, att_done.at(g, b) - 1)
                    nc.scalar.activation(mixed[:, n, :], ubank[:, :], ACT.Copy).then_inc(mix_read.sem, 1)

                for s in range(SLOTS):
                    b, h = divmod(s, ROW)
                    gb, bb = (g, 0) if b == 1 else (g - 1, 1)
                    if exists(gb):
                        for n in range(2):
                            if h == MIX_LAG + 8 * (n + 1):
                                evacuate(gb, bb, n)
                        if h in heads:
                            seconds.wait_full(act, gb, f"{bb}exp{h}")
                            act.wait_ge(mixing.sem, mixing.at(gb, f"{bb}head{h}") - NPR)
                            nc.scalar.activation(prob[:, h % NPR, :, :], seconds.bank(f"{bb}exp{h}")[:, :],
                                                 ACT.Exp, scale=float(HD) ** -0.5) \
                              .then_inc(seconds.reader(f"{bb}exp{h}"), 1)
                    if exists(g) and h == HEADS:
                        firsts.wait_full(act, g, f"{b}turn")
                        wait(act, max_stacked, (g * PAIR + b) * 32)
                        nc.scalar.activation(max_hi[:, :], firsts.bank(f"{b}turn")[0:HEADS, 0:SEQ], ACT.Copy,
                                             scale=-1 / SM).then_inc(max_high.sem, 1)
                    yield

            def tail_act(act, g, p, turn):
                def high_att(b):
                    act.wait_ge(att_done.sem, att_done.at(g, b))
                    nc.scalar.activation(att_hi[:, :, :], att[:, :, :], ACT.Copy).then_inc(att_high.sem, 1)

                def high_f(dt):
                    tail.wait_full(act, g, f"f{dt}")
                    nc.scalar.activation(xf_hi[:, dt, :], tail.bank(f"f{dt}")[:, :], ACT.Copy, scale=SX) \
                      .then_inc(tail_hi.sem, 1)

                def rectify(f):
                    tail.wait_full(act, g, f"up{f}")
                    act.wait_ge(hid_done.sem, hid_done.at(g, f) - 2)
                    nc.scalar.activation(relu[:, f % 2, :], tail.bank(f"up{f}")[:, :], ACT.Relu,
                                         scale=SF ** 0.5 / (SX * SW)).then_inc(tail.reader(f"up{f}"), 1)

                def high(f):
                    act.wait_ge(hid_done.sem, hid_done.at(g, f))
                    act.wait_ge(down_done.sem, down_done.at(g, f) - 2)
                    nc.scalar.activation(hid_hi[:, f % 2, :], hid[:, f % 2, :], ACT.Copy).then_inc(hid_hi_done.sem, 1)

                def drive_out():
                    act.wait_ge(down_done.sem, down_done.at(g, FC - 1))
                    act.wait_ge(fired.sem, fired.at(g, 0) - 1)
                    for n in range(2):
                        nc.scalar.activation(drive[:, n * 2 * D:(n + 1) * 2 * D], acc[n][:, :], ACT.Copy,
                                             scale=1 / (SW * SF)).then_inc(driven.sem, 1)

                def square(f):
                    tail.wait_read(act, g, f"up{f}")
                    act.wait_ge(hid_lo_done.sem, hid_lo_done.at(g, f) - 2)
                    nc.scalar.activation(hid[:, f % 2, :], relu[:, f % 2, :], ACT.Square).then_inc(hid_done.sem, 1)

                def load_x():
                    wait(act, x_out, HEAD + 16 * (g - 1))
                    act.dma_start(x_res[p][:, :, :], x_mid[g]).then_inc(res_in, 16)

                def store_x():
                    act.wait_ge(fired.sem, fired.at(g, 0))
                    act.dma_start(out[g], x_res[p][:, :, :]).then_inc(x_out, 16)

                yield from in_turn(turn, [(WO[0] - 3, load_x), (FIRED_AT + 1, store_x)]
                                   + [(DIVIDE[b] + 1, high_att, b) for b in range(PAIR)]
                                   + [(F_AT + 2 * dt, high_f, dt) for dt in range(DT)]
                                   + [(UP_AT + UP_STEP * f, rectify, f) for f in range(FC)]
                                   + [(UP_AT + UP_STEP * f + 1, square, f) for f in range(FC)]
                                   + [(UP_AT + UP_STEP * f + 2, high, f) for f in range(FC)]
                                   + [(DRIVE_AT, drive_out)])

            @block.scalar
            def _(act):
                groups(act, front_act, attention_act, tail_act)

            V = nc.vector

            def front_dve(dve, g, p):
                def low(step, hi, lo):
                    yield FRONT[step] + 1
                    low_of_bank(dve, front, front_hi, g, step, step, hi, lo, SX)

                def low_qk(first, s):
                    for m in range(2):
                        yield FRONT[f"{s}{m}"] + 1
                        dve.wait_ge(front_hi.sem, front_hi.at(g, f"{s}{m}"))
                        V.tensor_tensor(qk_lo[p][:, first + m, :], qk[:, m, :], qk_hi[p][:, first + m, :], ALU.subtract) \
                         .then_inc(front_lo.sem, 1)

                for dt in range(DT):
                    yield from low(f"ctx{dt}", ct_hi[:, dt, :], ct_lo[:, dt, :])
                yield FRONT["k0"]
                dve.wait_ge(x_in, 16 * (g + 1))
                moments_of(dve, norm, x_tok)
                yield from low_qk(0, "k")
                yield FRONT["k1"] + 1
                normalise(dve, norm, 0, rsqrt, g, x_tok)
                for dt in range(DT):
                    yield from low(f"x{dt}", xt_hi[:, dt, :], xt_lo[:, dt, :])
                yield from low_qk(2, "q")
                for n in range(2):
                    yield FRONT[f"v{n}"] + 1
                    front.wait_full(dve, g, f"v{n}")
                    if n == 0:
                        wait(dve, mixing.sem, mixing.at(g - 2, f"1head{HEADS - 1}"))
                    for half in range(2):
                        V.scalar_tensor_tensor(
                            out=v_one[p][:, 2 * n + half, :, 0:HD],
                            in0=front.bank(f"v{n}")[:, half * D:(half + 1) * D].rearrange("p (h d) -> p h d", h=HEADS),
                            scalar=1 / (SX * SW), in1=bias_v[:, :].rearrange("p (h d) -> p h d", h=HEADS),
                            op0=ALU.mult, op1=ALU.add).then_inc(values.sem, 1)
                    dve.wait_ge(values.sem, values.at(g, 2 * n + 1))
                    dve.sem_inc(front.reader(f"v{n}"), 1)

            def attention_dve(dve, g, p):
                for s in range(SLOTS):
                    b, h = divmod(s, ROW)
                    if exists(g) and h in heads:
                        firsts.wait_full(dve, g, f"{b}max{h}")
                        V.tensor_reduce(row_max[:, :, h], firsts.bank(f"{b}max{h}")[:, :].rearrange("p (q k) -> p q k", q=2),
                                        AX_X, ALU.max).then_inc(firsts.reader(f"{b}max{h}"), 1)
                    if exists(g) and h == HEADS:
                        low_of_bank(dve, firsts, max_high, g, f"{b}turn", f"{b}max", max_hi[:, :], max_lo[:, :],
                                    -1 / SM, cols=slice(0, SEQ), rows=slice(0, HEADS))
                    yield

            def tail_dve(dve, g, p, turn):
                xs = x_res[p][:, :, :].rearrange("p t d -> p (t d)")

                def invert(b):
                    dve.wait_ge(den_in, 16 * (g * PAIR + b + 1))
                    V.reciprocal(den_inv[:, :], den[:, :]).then_inc(inverted.sem, 1)

                def divide(b):
                    dve.wait_ge(inverse_in, 64 * (g * PAIR + b + 1))
                    dve.wait_ge(att_low.sem, att_low.at(g, b) - 1)
                    V.tensor_tensor(att[:, :, :], mixed[:, :, :], inverse[:, :, :], ALU.mult).then_inc(att_done.sem, 1)

                def low_att(b):
                    dve.wait_ge(att_high.sem, att_high.at(g, b))
                    V.tensor_tensor(att_lo[:, :, :].rearrange("p n q -> p (n q)"), att[:, :, :].rearrange("p n q -> p (n q)"),
                                    att_hi[:, :, :].rearrange("p n q -> p (n q)"), ALU.subtract).then_inc(att_low.sem, 1)

                def add_attention(b):
                    tail.wait_full(dve, g, f"wo{b}")
                    V.scalar_tensor_tensor(out=proj[:, :, :], in0=tail.bank(f"wo{b}")[:, :].rearrange("p (q d) -> p q d", q=2),
                                           scalar=1 / SW, in1=bias_o[:, :].unsqueeze(1).to_broadcast([P, 2, D]),
                                           op0=ALU.mult, op1=ALU.add).then_inc(tail.reader(f"wo{b}"), 1)
                    tail.wait_read(dve, g, f"wo{b}")
                    if b == 0:
                        dve.wait_ge(res_in, 16 * (g + 1))
                    rows = x_res[p][:, 2 * b:2 * b + 2, :]
                    V.scalar_tensor_tensor(out=rows, in0=proj[:, :, :], scalar=step_of[:, 2:3], in1=rows,
                                           op0=ALU.mult, op1=ALU.add).then_inc(x_mixed.sem, 1)

                def moments_f():
                    dve.wait_ge(x_mixed.sem, x_mixed.at(g, 1))
                    moments_of(dve, norm_f, x_res[p])

                def low_f(dt):
                    low_of_bank(dve, tail, tail_hi, g, f"f{dt}", f"f{dt}", xf_hi[:, dt, :], xf_lo[:, dt, :], SX)

                def low_hid(f):
                    dve.wait_ge(hid_hi_done.sem, hid_hi_done.at(g, f))
                    V.tensor_tensor(hid_lo[:, f % 2, :], hid[:, f % 2, :], hid_hi[:, f % 2, :], ALU.subtract) \
                     .then_inc(hid_lo_done.sem, 1)

                def integrate(k, c):
                    if k == 2:
                        dve.wait_ge(driven.sem, driven.at(g, c))
                    else:
                        dve.wait_ge(potential.sem, potential.at(g, (k - 1, c)))
                    cols = slice(c * 2 * D, (c + 1) * 2 * D)
                    before = drive if k == 2 else mem[(k - 1) % 2]
                    V.scalar_tensor_tensor(out=leak[:, cols], in0=before[:, cols], scalar=BETA, in1=drive[:, cols],
                                           op0=ALU.mult, op1=ALU.add)
                    dve.drain()
                    if k > 3:
                        dve.wait_ge(counted.sem, counted.at(g, (k - 2, c)))
                    V.scalar_tensor_tensor(out=mem[k % 2][:, cols], in0=before[:, cols], scalar=THRESHOLD,
                                           in1=leak[:, cols], op0=ALU.is_gt, op1=ALU.subtract, reverse1=True) \
                     .then_inc(potential.sem, 1)

                def add_spikes():
                    dve.wait_ge(counted.sem, counted.at(g, (STEPS, 1)))
                    V.scalar_tensor_tensor(out=xs, in0=spikes[:, :], scalar=step_of[:, 3:4], in1=xs,
                                           op0=ALU.mult, op1=ALU.add).then_inc(fired.sem, 1)

                yield from in_turn(turn, [(WO[b] + 1, add_attention, b) for b in range(PAIR)]
                                   + [(MIXED[b] + b, invert, b) for b in range(PAIR)]
                                   + [(DIVIDE[b], divide, b) for b in range(PAIR)]
                                   + [(DIVIDE[b] + 2, low_att, b) for b in range(PAIR)]
                                   + [(NORM, moments_f), (NORM + 1, normalise, dve, norm_f, 0, rsqrt_f, g, x_res[p])]
                                   + [(F_AT + 2 * dt + 1, low_f, dt) for dt in range(DT)]
                                   + [(UP_AT + UP_STEP * f + 3, low_hid, f) for f in range(FC)]
                                   + [(fire_slot(k, c), integrate, k, c) for k in range(2, STEPS + 1) for c in range(2)]
                                   + [(FIRED_AT, add_spikes)])

            @block.vector
            def _(dve):
                for t in v_one:
                    ins = V.memset(t[:, :, :, HD:], 1.0)
                ins.then_inc(preset, 1)

                def set_ones():
                    dve.wait_ge(zeroed, 4)
                    for t in k_stack:
                        V.memset(t[96:98, :, :], SM).then_inc(preset, 1)

                groups(dve, front_dve, attention_dve, tail_dve, set_ones)

            def power(pool, sig, rs, g):
                pool.wait_ge(sig.sem, sig.at(g, "var0"))
                nc.gpsimd.tensor_tensor(rstd[:, :], var_eps[:, :], minus_half[:, :], ALU.pow).then_inc(rs.sem, 1)

            def front_pool(pool, g, p):
                yield FRONT["k0"]
                power(pool, norm, rsqrt, g)

            def tail_pool(pool, g, p, turn):
                def count(k, c):
                    cols = slice(c * 2 * D, (c + 1) * 2 * D)
                    if k == 1:
                        pool.wait_ge(driven.sem, driven.at(g, c))
                        pool.sem_inc(pool_passed, 1)
                        pool.wait_ge(fired.sem, fired.at(g, 0) - 1)
                        pool.sem_inc(pool_passed, 1)
                        nc.gpsimd.tensor_scalar(spikes[:, cols], drive[:, cols], THRESHOLD, None, ALU.is_gt) \
                          .then_inc(counted.sem, 1)
                    else:
                        pool.wait_ge(counted.sem, counted.at(g, (k - 1, c)))
                        pool.sem_inc(pool_passed, 1)
                        pool.wait_ge(potential.sem, potential.at(g, (k, c)))
                        pool.sem_inc(pool_passed, 1)
                        nc.gpsimd.tensor_scalar(spike[:, cols], mem[k % 2][:, cols], THRESHOLD, None, ALU.is_gt) \
                          .then_inc(over.sem, 1)
                        pool.wait_ge(over.sem, over.at(g, (k, c)))
                        nc.gpsimd.tensor_tensor(spikes[:, cols], spikes[:, cols], spike[:, cols], ALU.add) \
                          .then_inc(counted.sem, 1)

                yield from in_turn(turn, [(NORM, power, pool, norm_f, rsqrt_f, g)]
                                   + [(DRIVE_AT + 1, count, 1, c) for c in range(2)]
                                   + [(fire_slot(k, c), count, k, c) for k in range(2, STEPS + 1) for c in range(2)])

            @block.gpsimd
            def _(pool):
                for s in heads_start:
                    pool.sem_inc(s.sem, HEAD)
                for s in (*firsts.read, *seconds.read, *front.read, *tail.read, x_out):
                    pool.sem_inc(s, HEAD)
                for t in (*q_stack, *k_stack):
                    nc.gpsimd.memset(t[:, :, :].bitcast(F32), 0.0).then_inc(zeroed, 1)
                pool.wait_ge(zeroed, 4)
                groups(pool, front_pool, lambda pool, g, p: iter(range(SLOTS)), tail_pool)



def kernel(**inputs):
    import concourse.bacc as _bacc
    from concourse.bass_utils import run_bass_kernel_spmd as _run

    a = {k: np.asarray(v) for k, v in inputs.items()}

    def tokens(v):
        return np.ascontiguousarray(v.reshape(GROUPS, TT, P, D).transpose(0, 2, 1, 3))

    def rows(w, cols=None):
        w = w if cols is None else w[:, cols]
        return w.reshape(DT, P, -1).transpose(1, 0, 2).reshape(P, -1)

    def up(w):
        return w.reshape(-1, P, DT, P).transpose(3, 0, 2, 1).reshape(P, -1)

    def down(w):
        return w.reshape(D, -1, P).transpose(2, 1, 0).reshape(P, -1)

    halves = np.concatenate([np.arange(0, D, 2), np.arange(1, D, 2)])
    by_place = np.arange(D).reshape(HEADS // 2, 2, HD).transpose(1, 2, 0).reshape(D)
    wo = a["L1_xattn_wo"].reshape(4, 4, HD, D).transpose(1, 2, 0, 3)
    wo_rows = np.zeros((4, 2 * HD, 4, D), np.float32)
    wo_rows[:, :HD] = wo
    packed = (
        [rows(a["L0_xattn_Wq"], halves), rows(a["L0_xattn_Wk"], halves), rows(a["L0_xattn_Wv"]),
         rows(a["L0_ffn_gate_w"].T),
         up(np.concatenate([a["L0_ffn_up_w"].reshape(EXPERTS * P, D), a["L0_ffn_shared_up_w"]])),
         a["L0_ffn_down_w"].transpose(2, 0, 1).reshape(P, -1), down(a["L0_ffn_shared_down_w"])],
        [rows(a["L1_xattn_wq"], by_place), rows(a["L1_xattn_wk"], by_place), rows(a["L1_xattn_wv"]),
         wo_rows.reshape(P, 4 * D), up(a["L1_ffn_W_fc"]), down(a["L1_ffn_W_proj"])],
    )
    for ws, n in zip(packed, WCOLS):
        ws.append(np.zeros((P, n - sum(w.shape[1] for w in ws)), np.float32))
    bqk = np.stack([a[n][by_place].reshape(2, P) for n in ("L1_xattn_bq", "L1_xattn_bk")]).reshape(4, P).T
    arrays = {
        "x": tokens(a["x"]), "ctx": tokens(a["ctx_1024"]),
        "gates": np.stack([a["g_xattn"], a["g_ffn"]], axis=1).reshape(4),
        "weights0": np.concatenate(packed[0], axis=1), "weights1": np.concatenate(packed[1], axis=1),
        "consts": constants(),
        "ebias": a["L0_ffn_e_bias"], "bqk": bqk, "bv": a["L1_xattn_bv"], "bo": a["L1_xattn_bo"],
    }
    arrays = {f"in_{k}": np.ascontiguousarray(v) for k, v in arrays.items()}
    nc = _bacc.Bacc("TRN2", target_bir_lowering=False, num_devices=1)
    aps = [nc.dram_tensor(k, v.shape, F32, kind="ExternalInput").ap() for k, v in arrays.items()]
    x_mid = nc.dram_tensor("x_mid", (GROUPS, P, TT, D), F32, kind="Internal").ap()
    out = nc.dram_tensor("out_x", (GROUPS, P, TT, D), F32, kind="ExternalOutput").ap()
    den_mid = nc.dram_tensor("den_mid", (PAIR, 4, 4 * SEQ), F32, kind="Internal").ap()
    build(nc, *aps, x_mid, den_mid, out)
    r = _run(nc, [arrays], core_ids=[0])
    got = r.results[0]["out_x"]
    return got.reshape(GROUPS, P, TT, D).transpose(0, 2, 1, 3).reshape(NB, SEQ, D)
```
